# Optimizing a Trainium2 kernel written in Bass

```python
import numpy as np
import jax
import jax.numpy as jnp

def _softmax(x, axis=-1):
    return jax.nn.softmax(x, axis=axis)

def _gelu(x):
    return jax.nn.gelu(x, approximate=True)

def _silu(x):
    return jax.nn.silu(x)

def _sigmoid(x):
    return jax.nn.sigmoid(x)

def _layernorm(x, axis=-1, eps=1e-05):
    m = jnp.mean(x, axis=axis, keepdims=True)
    v = jnp.var(x, axis=axis, keepdims=True)
    return (x - m) / jnp.sqrt(v + eps)

def _scatter_add(tgt, idx, src, axis=0):
    return tgt.at[idx].add(src)

def _segment_sum(src, seg, n):
    return jax.ops.segment_sum(src, seg, n)
kernel_name = 'mk_cond_resid_d2_seqx_r2_552d44'

def setup_inputs(seed: int=0):
    np.random.seed(seed)
    _w = jnp.asarray

    def _rec_inputs():
        import jax
        import jax.numpy as jnp
        _rk = jax.random.key(seed)
        x = -0.000125 + 0.9999 * jax.random.normal(jax.random.fold_in(_rk, 1), (4, 1024, 512), jnp.float32)
        _lenS = 1024 - jax.random.randint(jax.random.fold_in(_rk, 7), (4,), 0, max(1, 1024 // 4) + 1, jnp.int32)
        _lenS2 = 1024 - jax.random.randint(jax.random.fold_in(_rk, 8), (4,), 0, max(1, 1024 // 4) + 1, jnp.int32)
        itok_B_0_15 = jax.random.randint(jax.random.fold_in(_rk, 11), (4,), 0, 16, jnp.int32)
        itok_B_0_2 = jax.random.randint(jax.random.fold_in(_rk, 12), (4,), 0, 3, jnp.int32)
        return (x, itok_B_0_15, itok_B_0_2)
    x, itok_B_0_15, itok_B_0_2 = _rec_inputs()

    def _L0_cond_setup():
        import jax, jax.numpy as jnp
        import numpy as np
        B, N, DIM = (32, 512, 512)
        HID = 2048
        PART = 128
        OUT = 512
        SHARED = OUT - PART
        E = 16
        key = jax.random.key(seed)
        ks = jax.random.split(key, 8)
        s = 0.02
        return {'x': jax.random.normal(ks[0], (B, N, DIM), dtype=jnp.float32), 'indices': jax.random.randint(ks[1], (B,), 0, E, dtype=jnp.int64), 'fc1_w': jax.random.normal(ks[2], (HID, DIM), dtype=jnp.float32) * s, 'fc1_b': jnp.zeros((HID,), dtype=jnp.float32), 'fc2_w': jax.random.normal(ks[3], (SHARED, HID), dtype=jnp.float32) * s, 'fc2_b': jnp.zeros((SHARED,), dtype=jnp.float32), 'experts_w': jax.random.normal(ks[4], (E, PART, HID), dtype=jnp.float32) * s, 'experts_b': jnp.zeros((E, PART), dtype=jnp.float32)}
    _L0_cond_all = _L0_cond_setup()
    _L0_cond_in = {k: v for k, v in _L0_cond_all.items() if k in ('fc1_w', 'fc1_b', 'fc2_w', 'fc2_b', 'experts_w', 'experts_b')}
    del _L0_cond_all

    def _L1_cond_setup():
        import jax, jax.numpy as jnp
        import numpy as np
        NEG_INF = -1e+30
        key = jax.random.key(seed)
        k1, k2, k3, k4, k5 = jax.random.split(key, 5)
        B, S, D, A = (16, 512, 512, 128)
        hidden = jax.random.normal(k1, (B, S, D), dtype=jnp.float32)
        W1 = jax.random.normal(k2, (D, A), dtype=jnp.float32) / np.sqrt(D)
        b1 = jax.random.normal(k3, (A,), dtype=jnp.float32) * 0.01
        v = jax.random.normal(k4, (A,), dtype=jnp.float32) / np.sqrt(A)
        prompt_type_ids = jax.random.randint(k5, (B,), 0, 3, dtype=jnp.int32)
        return {'hidden': hidden, 'W1': W1, 'b1': b1, 'v': v, 'prompt_type_ids': prompt_type_ids}
    _L1_cond_all = _L1_cond_setup()
    _L1_cond_in = {k: v for k, v in _L1_cond_all.items() if k in ('W1', 'b1', 'v')}
    del _L1_cond_all
    return {'x': x, 'itok_B_0_15': itok_B_0_15, 'itok_B_0_2': itok_B_0_2, 'L0_cond_fc1_w': _L0_cond_in['fc1_w'], 'L0_cond_fc1_b': _L0_cond_in['fc1_b'], 'L0_cond_fc2_w': _L0_cond_in['fc2_w'], 'L0_cond_fc2_b': _L0_cond_in['fc2_b'], 'L0_cond_experts_w': _L0_cond_in['experts_w'], 'L0_cond_experts_b': _L0_cond_in['experts_b'], 'L1_cond_W1': _L1_cond_in['W1'], 'L1_cond_b1': _L1_cond_in['b1'], 'L1_cond_v': _L1_cond_in['v']}

def reference(x, itok_B_0_15, itok_B_0_2, L0_cond_fc1_w, L0_cond_fc1_b, L0_cond_fc2_w, L0_cond_fc2_b, L0_cond_experts_w, L0_cond_experts_b, L1_cond_W1, L1_cond_b1, L1_cond_v):
    import jax
    import jax.numpy as jnp

    def _L0_cond_ref(x, indices, fc1_w, fc1_b, fc2_w, fc2_b, experts_w, experts_b):
        import jax, jax.numpy as jnp
        import numpy as np
        B, N, DIM = (32, 512, 512)
        HID = 2048
        PART = 128
        OUT = 512
        SHARED = OUT - PART
        E = 16
        h = jax.nn.gelu(jnp.einsum('bnd,hd->bnh', x, fc1_w) + fc1_b, approximate=False)
        shared = jnp.einsum('bnh,sh->bns', h, fc2_w) + fc2_b
        We = experts_w[indices]
        be = experts_b[indices]
        expert_x = jnp.einsum('bnh,bph->bnp', h, We) + be[:, None, :]
        return jnp.concatenate([shared, expert_x], axis=-1)

    def _L1_cond_ref(hidden, W1, b1, v, prompt_type_ids):
        import jax, jax.numpy as jnp
        import numpy as np
        NEG_INF = -1e+30
        B, S, D = hidden.shape
        attn_in = jnp.tanh(jnp.einsum('bsd,da->bsa', hidden, W1) + b1)
        scores = jnp.einsum('bsa,a->bs', attn_in, v)
        idx = jnp.arange(S)
        j = idx[:, None]
        l = idx[None, :]
        prefix_m = l <= j
        postfix_m = l >= j
        cloze_m = l != j
        pt = prompt_type_ids[:, None, None]
        mask = jnp.where(pt == 0, prefix_m[None], jnp.where(pt == 1, postfix_m[None], cloze_m[None]))
        masked_scores = jnp.where(mask, scores[:, None, :], NEG_INF)
        p = jax.nn.softmax(masked_scores, axis=-1)
        cnt = jnp.sum(mask, axis=-1).astype(hidden.dtype)
        pooled = jnp.einsum('bjl,bld->bjd', p, hidden) / cnt[..., None]
        return pooled
    x = x + _L0_cond_ref(x, itok_B_0_15, L0_cond_fc1_w, L0_cond_fc1_b, L0_cond_fc2_w, L0_cond_fc2_b, L0_cond_experts_w, L0_cond_experts_b)
    x = x + _L1_cond_ref(x, L1_cond_W1, L1_cond_b1, L1_cond_v, itok_B_0_2)
    return x

_drawn_inputs = setup_inputs


def setup_inputs(seed=0):
    import zlib

    import numpy as np

    out = dict(_drawn_inputs(seed))
    spreads = {'L0_cond_fc1_b': (0.0, 0.1), 'L0_cond_fc2_b': (0.0, 0.1), 'L0_cond_experts_b': (0.0, 0.1)}
    factors = {}
    for name, (base, spread) in spreads.items():
        noise = np.random.default_rng([zlib.crc32(name.encode()), seed]).standard_normal(out[name].shape)
        drawn = base * np.exp(spread * noise) if base else spread * noise
        out[name] = jnp.asarray(drawn.astype(out[name].dtype))
    for name, factor in factors.items():
        out[name] = (out[name] * factor).astype(out[name].dtype)
    return out
```

```python
import concourse.bass as bass
from concourse import mybir
from contextlib import ExitStack

NB, SEQ, D = 4, 1024, 512
HID, SHARED, PART = 2048, 384, 128
A = 128
P = 128
TT = 512
HC, DC, OC = HID // P, D // P, D // P
CH = SEQ // P
CT = TT // P
NEG = -1.0e30
GROUPS = 4
RAW = 4

TRI = slice(0, P)
CROSS = slice(P, P + CH)
SEEN = slice(P + CH, P + 2 * CH)
CNT = slice(P + 2 * CH, P + 3 * CH)
NS, NP_, NC = P + 3 * CH, P + 3 * CH + 1, P + 3 * CH + 2
MW = P + 3 * CH + 4

R_FC1, R_FC2, R_EXP, R_B1, R_V = 0, HC, HC + SHARED // P, HC + SHARED // P + NB, HC + SHARED // P + NB + 1
NBR = R_V + 1


BANK = {"x", "w1", "w2", "xn", "attn", "score", "stats", "bc", "sums", "sums1", "den", "pool"}
LOADED = {"x", "w1", "w2"}
PROLOGUE = [("x", 0, 0, c) for c in range(CT)] + [("w1", 0), ("w1", 1)]


def tasks(kind, t, s):
    out = []
    if t == 1 or kind != "first":
        out += {0: [("ysum",)], 1: [("x1",)], 2: [("x1lo",), ("xn", 0)], 3: [("xn", 1), ("attn",)],
                4: [("xn", 2), ("score",)], 5: [("xn", 3)]}.get(s, [])
    if t == 0 and kind != "first":
        out += {5: [("stats",)], 7: [("bc", 0), ("bc", 1)], 8: [("exp",)], 9: [("sums",), ("sums1",)],
                10: [("den",)], 11: [("pool", 0)], 12: [("pool", 1)], 13: [("pool", 2), ("pool", 3)],
                14: [("pool", 4), ("pool", 5)], 15: [("pool", 6), ("pool", 7)]}.get(s, [])
    if kind == "tail":
        return out
    if kind == "first" and t == 0:
        if s == 0:
            out += [("bias",)]
            out += [("w2", ob, 0, 0) for ob in range(OC)]
        elif s < HC - 4:
            q, ob = (s + 3) // 4, (s - 1) % 4
            if ob < 3:
                out += [("w2", ob, q, 0)]
        if s + 2 < HC:
            out += [("w1", s + 2)]
    if t == 0 and s in (3, 7, 11):
        out += [("w2", OC - 1, (s + 1) // 4, 0)]
    if t == 1 and s == 12:
        out += [("w2", OC - 1, 0, 1)]
    if s in (5, 6, 8, 10):
        out += [("x", t, 1 - t, (5, 6, 8, 10).index(s))]
    return out


def body(kind):
    job = load = 0
    if kind == "first":
        job = load = len(PROLOGUE)
    out = []
    for t in range(2):
        for s in range(HC):
            row = []
            for task in tasks(kind, t, s):
                row.append((task, job, load))
                job += task[0] in BANK
                load += task[0] in LOADED
            out.append((t, s, row))
    return out, job, load


FIRST, J0, L0 = body("first")
LOOP, J, L = body("loop")
TAIL = [x for x in body("tail")[0] if x[0] == 0]
assert J % 2 == 0 and L % RAW == 0
BODIES = {"first": FIRST, "loop": LOOP, "tail": TAIL}


def job_of(kind, b, pos):
    return pos if kind == "first" else b * J + (J0 - J + pos)


def bank_of(kind, pos):
    return pos % 2 if kind == "first" else (J0 + pos) % 2


def bank_turn(kind, b, pos):
    return pos // 2 if kind == "first" else b * (J // 2) + ((J0 + pos) // 2 - J // 2)


def at(kind, t, task):
    return next(pos for tt, _, row in BODIES[kind] for k, pos, _ in row if tt == t and k == task)


def at_before(t, task):
    return at("loop", t, task) - J


def raw_of(kind, pos):
    return pos % RAW if kind == "first" else (L0 + pos) % RAW


def raw_turn(kind, b, pos):
    return pos // RAW if kind == "first" else b * (L // RAW) + ((L0 + pos) // RAW - L // RAW)


def build(nc, x, tok_e, tok_t, fc1_w, fc1_b, fc2_w, fc2_b, exp_w, exp_b, W1, b1, v, out):
    f32, f32r, i32 = mybir.dt.float32, mybir.dt.float32r, mybir.dt.int32
    ALU, ACT, AX = mybir.AluOpType, mybir.ActivationFunctionType, mybir.AxisListType

    ctx = ExitStack()
    with ctx:
        def sb(name, shape, dt=f32):
            return ctx.enter_context(nc.sbuf_tensor(name, shape, dt))

        def pb(name):
            return ctx.enter_context(nc.psum_tensor(name, [P, 512], f32))

        def sem(name):
            return ctx.enter_context(nc.semaphore(name))

        w1T = sb("w1T", [P, HC, D])
        w2T = sb("w2T", [P, HC, D])
        w1h, w1l = sb("w1h", [P, 2, D], f32r), sb("w1l", [P, 2, D], f32r)
        w2h, w2l = sb("w2h", [P, 2, D], f32r), sb("w2l", [P, 2, D], f32r)
        xh = [sb(f"xh{i}", [P, DC, TT], f32r) for i in range(2)]
        xl = [sb(f"xl{i}", [P, DC, TT], f32r) for i in range(2)]
        x1T = sb("x1T", [P, OC, TT])
        raw = sb("raw", [P, RAW, 512])
        g = sb("g", [P, 2, TT])
        hh, hl = sb("hh", [P, 2, TT], f32r), sb("hl", [P, 2, TT], f32r)
        xnh, xnl = sb("xnh", [P, CH, D], f32r), sb("xnl", [P, CH, D], f32r)
        W1h, W1l = sb("W1h", [P, DC, A], f32r), sb("W1l", [P, DC, A], f32r)
        Ph, Pl = sb("Ph", [P, CH, P], f32r), sb("Pl", [P, CH, P], f32r)
        Ws = sb("Ws", [P, CH, P], f32r)
        E4 = sb("E4", [P, CH, P], f32r)
        Bs = sb("Bs", [P, D], f32r)
        B1s = sb("B1s", [P, 2], f32r)
        oo = sb("oo", [P, 2, D])
        ident = sb("ident", [P, P])
        ones2 = sb("ones2", [P, 2], f32r)
        ones8 = sb("ones8", [CH, P])
        rep = sb("rep", [CH, GROUPS, 32])
        K0, KS, KP, KC = (sb(n, [P, MW]) for n in ("K0", "KS", "KP", "KC"))
        kt = sb("kt", [P, MW])
        TM = sb("TM", [P, MW])
        ty = sb("ty", [P, 1], i32)
        tyf = sb("tyf", [P, 4])
        cnti = sb("cnti", [P, 2 * CH], i32)
        brow = sb("brow", [NBR, P])
        bcol = sb("bcol", [P, NBR])
        vz = sb("vz", [P, CH, CH])
        s8a, s8 = sb("s8a", [CH, P]), sb("s8", [CH, P])
        F8, G8 = sb("F8", [CH, P + 1]), sb("G8", [CH, P + 1])
        DG = sb("DG", [CH, CH])
        st = sb("st", [P, 2 * CH + 1])
        t88, m0 = sb("t88", [CH, CH]), sb("m0", [CH, P])
        mc = sb("mc", [CH, 1])
        m8 = sb("m8", [CH, P])
        Ef = sb("Ef", [P, CH])
        rd = sb("rd", [P, CH])

        Pf = x1T[:, 0:2, :].rearrange("p a n -> p (a n)")
        th = oo[:, 0, :]
        Wf = x1T[:, 2:4, :].rearrange("p a n -> p (a n)")

        yb = [pb(f"y{i}") for i in range(OC)]
        hb = [pb(f"h{i}") for i in range(2)]
        jb = [pb(f"j{i}") for i in range(2)]

        raw_in = [sem(f"raw_in{i}") for i in range(RAW)]
        bias_in, W1_in, type_in = sem("bias_in"), sem("W1_in"), sem("type_in")
        out_put = [sem(f"out_put{i}") for i in range(2)]
        const_done, mask_done = sem("const_done"), sem("mask_done")
        gstep = sem("gstep")
        bias_turned, bcol_done, vz_done = sem("bias_turned"), sem("bcol_done"), sem("vz_done")
        job_done = sem("job_done")
        bank_read = [sem(f"bank_read{i}") for i in range(2)]
        fc1_done, fc2_done = sem("fc1_done"), sem("fc2_done")
        w1hi, w1lo, w2hi, w2lo = sem("w1hi"), sem("w1lo"), sem("w2hi"), sem("w2lo")
        W1hi, W1lo = sem("W1hi"), sem("W1lo")
        gelu_done, hhi, hlo = sem("gelu_done"), sem("hhi"), sem("hlo")
        xhi, xnhi = sem("xhi"), sem("xnhi")
        ysum, x1_done, x1hi, x1lo = sem("ysum"), sem("x1_done"), sem("x1hi"), sem("x1lo")
        chain = sem("chain")
        exp_done = sem("exp_done")
        passed = sem("passed")
        Ehi, Elo = sem("Ehi"), sem("Elo")
        PWhi, Plo, Wlo = sem("PWhi"), sem("Plo"), sem("Wlo")
        sumhi = sem("sumhi")
        rd_done, row_sum = sem("rd_done"), sem("row_sum")

        NCHAIN, DIAG = 10, 3

        def wait(eng, s, value):
            if not (isinstance(value, int) and value <= 0):
                eng.wait_ge(s, value)

        def wait_used(eng, kind, b, pos):
            eng.wait_ge(bank_read[bank_of(kind, pos)], bank_turn(kind, b, pos) + 1)

        def gate(eng, s, value):
            wait(eng, s, value)
            eng.sem_inc(passed, 1)

        def run(eng, part):
            part("first", 0)
            with eng.Fori(1, NB) as b:
                part("loop", b)
            part("tail", NB)

        def slot_no(b, t, s):
            return b * 2 * HC + (t * HC + s)

        def tile_before(b, t):
            return b * 2 + (t - 1)

        def batch_of(ap, b):
            return ap[bass.ds(b, 1)]

        block = ctx.enter_context(nc.Block())

        @block.sync
        def _(sp):
            order = {k: [r[0] for _, _, row in BODIES[k] for r in row if r[0][0] in LOADED] for k in ("first", "loop")}
            order["first"] = PROLOGUE + order["first"]

            def source(task, b):
                if task[0] == "x":
                    _, ahead, t, c = task
                    rows = batch_of(x, (b + ahead) % NB)
                    return rows[:, t * TT + c * P:t * TT + (c + 1) * P, :].rearrange("o p n -> (o p) n")
                if task[0] == "w1":
                    return fc1_w[task[1] * P:(task[1] + 1) * P, :]
                _, ob, q, ahead = task
                if ob < OC - 1:
                    return fc2_w[ob * P:(ob + 1) * P, q * 512:(q + 1) * 512]
                e = sp.value_load(batch_of(tok_e, (b + ahead) % NB).rearrange("(o n) -> o n", o=1),
                                  min_val=0, max_val=exp_w.shape[0] - 1)
                return batch_of(exp_w, e)[:, :, q * 512:(q + 1) * 512].rearrange("o p n -> (o p) n")

            def load(kind, b, n):
                slot = raw_of(kind, n)
                sp.dma_start(raw[:, slot, :], source(order[kind][n], b)).then_inc(raw_in[slot], 16)

            def follow(kind, b, pos, n):
                gate(sp, job_done, job_of(kind, b, pos) + 1)
                if n + RAW < len(order[kind]):
                    load(kind, b, n + RAW)
                else:
                    load("loop", b + 1, n + RAW - len(order[kind]))

            def part(kind, b):
                if kind != "first":
                    gate(sp, mask_done, b - 1)
                    sp.dma_start(ty[:, :], batch_of(tok_t, b - 1).rearrange("(o n) -> o n", o=1).to_broadcast([P, 1])
                                 ).then_inc(type_in, 16)
                for t, s, row in BODIES[kind]:
                    for task, pos, n in row:
                        if task[0] in LOADED:
                            follow(kind, b, pos, n)
                        if task[0] == "pool":
                            c = task[1]
                            gate(sp, row_sum, b * CH + (c + 1 - CH))
                            sp.dma_start(batch_of(out, b - 1)[:, c * P:(c + 1) * P, :].rearrange("o p n -> (o p) n"),
                                         oo[:, c % 2, :]).then_inc(out_put[c % 2], 16)

            for n in range(RAW):
                load("first", 0, n)
            for n in range(len(PROLOGUE)):
                follow("first", 0, n, n)
                if n == 1:
                    sp.dma_start(x1T[:, 0, :].rearrange("p (c a) -> p c a", c=DC),
                                 W1.rearrange("(c p) a -> p c a", p=P)).then_inc(W1_in, 16)
            run(sp, part)
            for i in range(2):
                sp.wait_ge(out_put[i], 16 * NB * CH // 2)
            for i in range(RAW):
                sp.wait_ge(raw_in[i], 16 * len([n for n in range(L0 + (NB - 1) * L + RAW) if n % RAW == i]))

        @block.gpsimd
        def _(pool):
            steps = [0]

            def link(ins):
                steps[0] += 1
                ins.then_inc(gstep, 1)
                pool.wait_ge(gstep, steps[0])

            def mark(ap, coef, count, cm, base=0, equal=False, fill=NEG):
                k = 1 if equal else -1
                return nc.gpsimd.affine_select(
                    out=ap, in_=ap, compare_op=ALU.not_equal if equal else ALU.is_ge, fill=fill,
                    base=k * base, pattern=[[k * coef, count]], channel_multiplier=k * cm)

            link(nc.gpsimd.memset(ident[:, :], 0.0))
            mark(ident[:, :], -1, P, 1, equal=True, fill=1.0).then_inc(const_done, 1)
            pool.wait_ge(const_done, 1)
            for r, src in ((R_FC1, fc1_b), (R_FC2, fc2_b), (R_B1, b1), (R_V, v)):
                pool.dma_start(brow[r:r + src.shape[0] // P, :], src.rearrange("(c p) -> c p", p=P)).then_inc(bias_in, 16)
            for b in range(NB):
                e = pool.value_load(tok_e[b:b + 1].rearrange("(o n) -> o n", o=1), min_val=0, max_val=exp_b.shape[0] - 1)
                pool.dma_start(brow[R_EXP + b:R_EXP + b + 1, :], batch_of(exp_b, e)).then_inc(bias_in, 16)
            link(nc.gpsimd.memset(ones8[:, :], 1.0))
            link(nc.gpsimd.memset(ones2[:, :].bitcast(f32), 1.0))
            link(nc.gpsimd.memset(vz[:, :, :], 0.0))
            link(nc.gpsimd.memset(E4[:, :, :].bitcast(f32), 0.0))
            link(nc.gpsimd.memset(F8[:, :], NEG))
            link(nc.gpsimd.memset(G8[:, :], NEG))
            for tile in (K0, KS, KP):
                link(nc.gpsimd.memset(tile[:, :], 0.0))
            link(nc.gpsimd.memset(KC[:, :], 0.0))
            for gr in range(GROUPS):
                link(nc.gpsimd.tensor_copy(rep[:, gr, :], ident[0:CH, 0:32]))
            link(mark(KS[:, TRI], 1, P, -1))
            link(mark(KP[:, TRI], -1, P, 1))
            link(mark(KC[:, TRI], -1, P, 1, equal=True))
            for gr in range(GROUPS):
                rows = slice(32 * gr, 32 * gr + 32)
                link(mark(KS[rows, CROSS], 1, CH, -1))
                link(mark(KP[rows, CROSS], -1, CH, 1))
                link(mark(K0[rows, CROSS], -1, CH, 1, equal=True))
                link(mark(K0[rows, CROSS], 0, CH, 1, base=1 - CH))
            link(mark(KS[:, SEEN], -1, CH, 1))
            link(mark(KP[:, SEEN], 1, CH, -1))
            link(mark(K0[:, SEEN], -1, CH, 1, equal=True))
            link(nc.gpsimd.memset(KS[:, NS:NS + 1], NEG))
            link(nc.gpsimd.memset(KP[:, NP_:NP_ + 1], NEG))
            link(nc.gpsimd.memset(KC[:, NC:NC + 1], NEG))
            link(nc.gpsimd.memset(KC[:, CNT], float(SEQ - 1)))
            link(nc.gpsimd.iota(cnti[:, 0:CH], pattern=[[-P, CH]], base=SEQ, channel_multiplier=-1))
            link(nc.gpsimd.iota(cnti[:, CH:2 * CH], pattern=[[P, CH]], base=1, channel_multiplier=1))
            link(nc.gpsimd.tensor_copy(KS[:, CNT], cnti[:, 0:CH]))
            link(nc.gpsimd.tensor_copy(KP[:, CNT], cnti[:, CH:2 * CH]))
            nc.gpsimd.memset(kt[:, 0:1], 0.0).then_inc(const_done, 1)
            before_masks, per_mask = steps[0], 10

            def part(kind, b):
                if kind == "first":
                    return
                made = [0]

                def then(ins):
                    made[0] += 1
                    ins.then_inc(gstep, 1)
                    gate(pool, gstep, b * per_mask + (before_masks - per_mask + made[0]))

                pool.wait_ge(type_in, b * 16)
                gate(pool, rd_done, b - 1)
                then(nc.gpsimd.tensor_copy(tyf[:, 0:1], ty[:, :]))
                then(nc.gpsimd.tensor_scalar(tyf[:, 1:2], tyf[:, 0:1], 0.0, None, ALU.is_equal))
                then(nc.gpsimd.tensor_scalar(tyf[:, 2:3], tyf[:, 0:1], 1.0, None, ALU.is_equal))
                then(nc.gpsimd.tensor_tensor(tyf[:, 3:4], tyf[:, 1:2], tyf[:, 2:3], ALU.add))
                then(nc.gpsimd.tensor_scalar(tyf[:, 3:4], tyf[:, 3:4], -1.0, 1.0, ALU.mult, ALU.add))
                then(nc.gpsimd.tensor_scalar(kt[:, :], KS[:, :], tyf[:, 2:3], None, ALU.mult))
                then(nc.gpsimd.tensor_scalar(TM[:, :], KP[:, :], tyf[:, 1:2], None, ALU.mult))
                then(nc.gpsimd.tensor_tensor(TM[:, :], TM[:, :], kt[:, :], ALU.add))
                then(nc.gpsimd.tensor_scalar(kt[:, :], KC[:, :], tyf[:, 3:4], None, ALU.mult))
                then(nc.gpsimd.tensor_tensor(TM[:, :], TM[:, :], kt[:, :], ALU.add))
                nc.gpsimd.tensor_tensor(TM[:, :], TM[:, :], K0[:, :], ALU.add).then_inc(mask_done, 1)
                for t, s, row in BODIES[kind]:
                    for task, pos, _ in row:
                        if task[0] == "pool":
                            c = task[1]
                            wait_used(pool, kind, b, pos)
                            nc.gpsimd.tensor_tensor(oo[:, c % 2, :], oo[:, c % 2, :], xnl[:, c, :].bitcast(f32),
                                                    ALU.add).then_inc(row_sum, 1)

            run(pool, part)

        @block.tensor
        def _(pe):
            def three(ps, ah, al, bh, bl, first, last):
                nc.tensor.matmul(ps, ah, bh, start=first, stop=False)
                nc.tensor.matmul(ps, ah, bl, start=False, stop=False)
                return nc.tensor.matmul(ps, al, bh, start=False, stop=last)

            def fc1(kind, b, t, s):
                ring, S = s % 2, slot_no(b, t, s)
                if s == 0:
                    last_chunk = (at(kind, 0, ("x", 0, 1, CT - 1)) if t == 1 else
                                  CT - 1 if kind == "first" else at_before(1, ("x", 1, 0, CT - 1)))
                    wait_used(pe, kind, b, last_chunk)
                pe.wait_ge(w1lo, S + 1)
                wait(pe, gelu_done, S - 1)
                for dc in range(DC):
                    w = slice(dc * P, (dc + 1) * P)
                    last = three(hb[ring][:, :], w1h[:, ring, w], w1l[:, ring, w], xh[t][:, dc, :], xl[t][:, dc, :],
                                 dc == 0, dc == DC - 1)
                last.then_inc(fc1_done, 1)

            def fc2(b, t, s):
                ring, S = s % 2, slot_no(b, t, s)
                pe.wait_ge(w2lo, S + 1)
                pe.wait_ge(hlo, S + 1)
                for oc in range(OC):
                    if s == 0:
                        wait(pe, ysum, tile_before(b, t) * OC + (oc + 1))
                    w = slice(oc * P, (oc + 1) * P)
                    three(yb[oc][:, :], w2h[:, ring, w], w2l[:, ring, w], hh[:, ring, :], hl[:, ring, :],
                          s == 0, s == HC - 1).then_inc(fc2_done, 1)

            def job(kind, b, t, task, pos, n):
                bank = jb[bank_of(kind, pos)]
                T1 = tile_before(b, t)
                wait(pe, bank_read[bank_of(kind, pos)], bank_turn(kind, b, pos))
                if task[0] in LOADED:
                    r = raw_of(kind, n)
                    pe.wait_ge(raw_in[r], raw_turn(kind, b, n) * 16 + 16)
                    for i in range(4):
                        last = nc.tensor.transpose(bank[:, i * P:(i + 1) * P], raw[:, r, i * P:(i + 1) * P], ident[:, :])
                elif task[0] == "xn":
                    c = task[1]
                    pe.wait_ge(x1_done, T1 * OC + OC)
                    for i in range(OC):
                        last = nc.tensor.transpose(bank[:, i * P:(i + 1) * P], x1T[:, i, c * P:(c + 1) * P], ident[:, :])
                elif task[0] == "attn":
                    if kind == "first":
                        pe.wait_ge(W1lo, 1)
                    pe.wait_ge(x1lo, T1 * OC + OC)
                    for dc in range(DC):
                        last = three(bank[:, :], W1h[:, dc, :], W1l[:, dc, :], xh[1 - t][:, dc, :], xl[1 - t][:, dc, :],
                                     dc == 0, dc == DC - 1)
                elif task[0] == "score":
                    wait_used(pe, kind, b, at(kind, t, ("attn",)))
                    if kind == "first":
                        pe.wait_ge(vz_done, 1)
                    for i in range(CT):
                        last = nc.tensor.matmul(bank[0:CH, 0:P], vz[:, (1 - t) * CT + i, :], th[:, i * P:(i + 1) * P],
                                                start=(i == 0), stop=(i == CT - 1))
                elif task[0] == "stats":
                    pe.wait_ge(chain, b * NCHAIN + (DIAG - NCHAIN))
                    nc.tensor.matmul(bank[:, CH:2 * CH], ones8[:, :], DG[:, :], start=True, stop=True)
                    nc.tensor.transpose(bank[:, 0:CH], s8[:, :], ident[0:CH, 0:CH])
                    last = nc.tensor.matmul(bank[:, 2 * CH:2 * CH + 1], rep[:, :, :].rearrange("c g k -> c (g k)"),
                                            F8[:, P:P + 1], start=True, stop=True)
                elif task[0] == "bc":
                    pe.wait_ge(chain, b * NCHAIN)
                    for i in range(CT):
                        c = task[1] * CT + i
                        last = nc.tensor.matmul(bank[:, i * P:(i + 1) * P], ident[0:CH, c:c + 1].to_broadcast([CH, P]),
                                                m8[:, :], start=True, stop=True)
                elif task[0] == "sums":
                    pe.wait_ge(Elo, b)
                    wait_used(pe, kind, b, at(kind, t, ("xn", CT - 1)))
                    for c in range(CH):
                        nc.tensor.matmul(bank[:, :], E4[:, c, :], xnh[:, c, :], start=(c == 0), stop=False)
                        last = nc.tensor.matmul(bank[:, :], E4[:, c, :], xnl[:, c, :], start=False, stop=(c == CH - 1))
                elif task[0] == "sums1":
                    for c in range(CH):
                        last = nc.tensor.matmul(bank[:, 0:2], E4[:, c, :], ones2[:, :], start=(c == 0), stop=(c == CH - 1))
                elif task[0] == "den":
                    pe.wait_ge(Plo, b)
                    pe.wait_ge(Wlo, b)
                    wait_used(pe, kind, b, at(kind, t, ("sums1",)))
                    for c in range(CH):
                        two = bank[:, 2 * c:2 * c + 2]
                        nc.tensor.matmul(two, Ph[:, c, :], ones2[:, :], start=True, stop=False)
                        nc.tensor.matmul(two, Pl[:, c, :], ones2[:, :], start=False, stop=False)
                        last = nc.tensor.matmul(two, Ws[:, c, :], B1s[:, :], start=False, stop=True)
                elif task[0] == "pool":
                    c = task[1]
                    three(bank[:, :], Ph[:, c, :], Pl[:, c, :], xnh[:, c, :], xnl[:, c, :], True, False)
                    last = nc.tensor.matmul(bank[:, :], Ws[:, c, :], Bs[:, :], start=False, stop=True)
                last.then_inc(job_done, 1)

            def part(kind, b):
                for t, s, row in BODIES[kind]:
                    if kind != "tail":
                        fc1(kind, b, t, s)
                    elif s == 0:
                        fc2(b - 1, 1, HC - 1)
                    for task, pos, n in row:
                        if task[0] == "bias":
                            pe.wait_ge(bias_in, 16 * (4 + NB))
                            nc.tensor.transpose(yb[0][:, 0:NBR], brow[:, :], ident[0:NBR, 0:NBR]).then_inc(bias_turned, 1)
                        elif task[0] in BANK:
                            job(kind, b, t, task, pos, n)
                    if kind != "tail":
                        if s > 0:
                            fc2(b, t, s - 1)
                        elif t == 1:
                            fc2(b, 0, HC - 1)
                        elif kind != "first":
                            fc2(b - 1, 1, HC - 1)

            pe.wait_ge(const_done, 1)
            for n, task in enumerate(PROLOGUE):
                job("first", 0, 0, task, n, n)
            run(pe, part)

        @block.scalar
        def _(act):
            def hi(out_, in_):
                return nc.scalar.activation(out_, in_, ACT.Copy)

            def split_w1(kind, b, t, s):
                nxt, S1 = (s + 1) % HC, slot_no(b, t, s + 1)
                if kind == "first" and t == 0 and nxt:
                    wait_used(act, kind, b, PROLOGUE.index(("w1", nxt)) if nxt < 2 else at(kind, 0, ("w1", nxt)))
                wait(act, fc1_done, S1 - 1)
                hi(w1h[:, nxt % 2, :], w1T[:, nxt, :]).then_inc(w1hi, 1)

            def split_w2(kind, b, t, s):
                if t == 0 and s % 4 == 0:
                    if kind == "loop" and s == 0:
                        wait_used(act, kind, b, at_before(1, ("w2", OC - 1, 0, 1)))
                    else:
                        wait_used(act, kind, b, at(kind, 0, ("w2", OC - 1, s // 4, 0)))
                wait(act, fc2_done, (slot_no(b, t, s) - 2) * OC + OC)
                hi(w2h[:, s % 2, :], w2T[:, s, :]).then_inc(w2hi, 1)

            def task_part(kind, b, t, task, pos):
                T1 = tile_before(b, t)
                bank = jb[bank_of(kind, pos)]
                if task[0] in ("x", "xn", "attn", "sums", "sums1"):
                    act.wait_ge(job_done, job_of(kind, b, pos) + 1)
                if task[0] == "x":
                    _, _, tt, c = task
                    hi(xh[tt][:, :, c * P:(c + 1) * P], bank[:, :].rearrange("p (d n) -> p d n", d=DC)).then_inc(xhi, 1)
                elif task[0] == "x1":
                    for oc in range(OC):
                        act.wait_ge(x1_done, T1 * OC + (oc + 1))
                        hi(xh[1 - t][:, oc, :], x1T[:, oc, :]).then_inc(x1hi, 1)
                elif task[0] == "xn":
                    if task[1] == 0 and t == 1 and kind == "loop":
                        wait_used(act, kind, b, at(kind, 0, ("pool", CH - 1)))
                    hi(xnh[:, (1 - t) * CT + task[1], :], bank[:, :]).then_inc(xnhi, 1)
                elif task[0] == "attn":
                    if t == 1 and kind == "loop":
                        act.wait_ge(out_put[0], b * (16 * CH // 2))
                    nc.scalar.activation(th[:, :], bank[:, :], ACT.Tanh, bias=bcol[:, R_B1:R_B1 + 1]
                                         ).then_inc(bank_read[bank_of(kind, pos)], 1)
                elif task[0] == "exp":
                    wait_used(act, kind, b, at(kind, t, ("bc", 1)))
                    for tile in (Ef[:, :], Pf, Wf):
                        nc.scalar.activation(tile, tile, ACT.Exp).then_inc(exp_done, 1)
                    for i, (part_, full) in enumerate(((Ph, Pf), (Ws, Wf))):
                        act.wait_ge(exp_done, b * 3 - 1 + i)
                        hi(part_[:, :, :].rearrange("p c n -> p (c n)"), full).then_inc(PWhi, 1)
                elif task[0] == "sums":
                    hi(Bs[:, :], bank[:, :]).then_inc(sumhi, 1)
                elif task[0] == "sums1":
                    hi(B1s[:, :], bank[:, 0:2]).then_inc(sumhi, 1)

            def part(kind, b):
                for t, s, row in BODIES[kind]:
                    if kind != "tail":
                        S, ring = slot_no(b, t, s), s % 2
                        split_w1(kind, b, t, s)
                        act.wait_ge(fc1_done, S + 1)
                        wait(act, hlo, S - 1)
                        if kind == "first" and t == 0 and s == 0:
                            act.wait_ge(bcol_done, 1)
                        nc.scalar.activation(g[:, ring, :], hb[ring][:, :], ACT.Gelu,
                                             bias=bcol[:, R_FC1 + s:R_FC1 + s + 1]).then_inc(gelu_done, 1)
                        wait(act, fc2_done, (S - 2) * OC + OC)
                        act.wait_ge(gelu_done, S + 1)
                        hi(hh[:, ring, :], g[:, ring, :]).then_inc(hhi, 1)
                        if kind != "first" or t == 1:
                            split_w2(kind, b, t, s)
                    for task, pos, _ in row:
                        task_part(kind, b, t, task, pos)
                    if kind == "first" and t == 0:
                        split_w2(kind, b, t, s)

            for n, task in enumerate(PROLOGUE):
                task_part("first", 0, 0, task, n)
            wait_used(act, "first", 0, PROLOGUE.index(("w1", 0)))
            hi(w1h[:, 0, :], w1T[:, 0, :]).then_inc(w1hi, 1)
            act.wait_ge(W1_in, 16)
            hi(W1h[:, :, :].rearrange("p c a -> p (c a)"), x1T[:, 0, :]).then_inc(W1hi, 1)
            run(act, part)

        @block.vector
        def _(dve):
            def lo(out_, in_, hi_):
                return nc.vector.tensor_tensor(out_, in_, hi_.bitcast(f32), ALU.subtract)

            def task_part(kind, b, t, task, pos):
                T1 = tile_before(b, t)
                bk = bank_of(kind, pos)
                bank, used = jb[bk], bank_read[bk]
                if task[0] in ("w1", "w2", "score", "stats", "bc", "den", "pool"):
                    dve.wait_ge(job_done, job_of(kind, b, pos) + 1)
                if task[0] == "x":
                    _, _, tt, c = task
                    in_prologue = kind == "first" and pos < len(PROLOGUE)
                    dve.wait_ge(xhi, c + 1 if in_prologue else b * 2 * CT + ((t + 1) * CT + c + 1))
                    where = (slice(None), slice(None), slice(c * P, (c + 1) * P))
                    lo(xl[tt][where], bank[:, :].rearrange("p (d n) -> p d n", d=DC), xh[tt][where]).then_inc(used, 1)
                elif task[0] == "w1":
                    nc.vector.tensor_copy(w1T[:, task[1], :], bank[:, :]).then_inc(used, 1)
                elif task[0] == "w2":
                    _, ob, q, _ = task
                    nc.vector.tensor_copy(w2T[:, 4 * q:4 * q + 4, ob * P:(ob + 1) * P],
                                          bank[:, :].rearrange("p (d n) -> p d n", d=4)).then_inc(used, 1)
                elif task[0] == "ysum":
                    for oc in range(OC):
                        shared = oc < OC - 1
                        bias = (bcol[:, R_FC2 + oc:R_FC2 + oc + 1] if shared else
                                bcol[:, bass.ds(b + (R_EXP + t - 1), 1)])
                        dve.wait_ge(fc2_done, T1 * HC * OC + ((HC - 1) * OC + oc + 1))
                        nc.vector.scalar_tensor_tensor(x1T[:, oc, :], yb[oc][:, :], bias, xh[1 - t][:, oc, :].bitcast(f32),
                                                       ALU.add, ALU.add).then_inc(ysum, 1)
                elif task[0] == "x1":
                    for oc in range(OC):
                        dve.wait_ge(ysum, T1 * OC + (oc + 1))
                        nc.vector.tensor_tensor(x1T[:, oc, :], x1T[:, oc, :], xl[1 - t][:, oc, :].bitcast(f32),
                                                ALU.add).then_inc(x1_done, 1)
                elif task[0] == "x1lo":
                    for oc in range(OC):
                        dve.wait_ge(x1hi, T1 * OC + (oc + 1))
                        lo(xl[1 - t][:, oc, :], x1T[:, oc, :], xh[1 - t][:, oc, :]).then_inc(x1lo, 1)
                elif task[0] == "xn":
                    c = (1 - t) * CT + task[1]
                    dve.wait_ge(xnhi, T1 * CT + (task[1] + 1))
                    if task[1] == 0 and t == 1 and kind == "loop":
                        dve.wait_ge(row_sum, b * CH)
                    lo(xnl[:, c, :], bank[:, :], xnh[:, c, :]).then_inc(used, 1)
                elif task[0] == "score":
                    if t == 1:
                        nc.vector.tensor_copy(s8a[:, :], bank[0:CH, 0:P]).then_inc(used, 1)
                    else:
                        nc.vector.tensor_tensor(s8[:, :], bank[0:CH, 0:P], s8a[:, :], ALU.add).then_inc(used, 1)
                        wait_used(dve, kind, b, pos)
                        maxima(b)
                elif task[0] == "stats":
                    nc.vector.tensor_copy(st[:, :], bank[:, 0:2 * CH + 1]).then_inc(used, 1)
                    dve.wait_ge(mask_done, b)
                    wait_used(dve, kind, b, pos)
                    row_maxima(b)
                elif task[0] == "bc":
                    for i in range(CT):
                        c = task[1] * CT + i
                        nc.vector.scalar_tensor_tensor(Pf[:, c * P:(c + 1) * P], bank[:, i * P:(i + 1) * P], st[:, c:c + 1],
                                                       TM[:, TRI], ALU.add, ALU.add)
                    half = slice(task[1] * TT, (task[1] + 1) * TT)
                    cross = TM[:, P + task[1] * CT:P + (task[1] + 1) * CT]
                    nc.vector.scalar_tensor_tensor(
                        Wf[:, half].rearrange("p (c n) -> p c n", c=CT), bank[:, :].rearrange("p (c n) -> p c n", c=CT),
                        st[:, 2 * CH:2 * CH + 1], cross.unsqueeze(2).to_broadcast([P, CT, P]), ALU.add, ALU.add
                    ).then_inc(used, 1)
                elif task[0] == "exp":
                    diagonal = E4[:, :, :].rearrange("p c n -> p (c n)")
                    dve.wait_ge(exp_done, b * 3 - 2)
                    for gr in range(GROUPS - 1):
                        last = nc.vector.tensor_copy(diagonal[:, 32 * gr:32 * gr + (CH - 1) * (P + 1) + 1:P + 1], Ef[:, :])
                    last.then_inc(Ehi, 1)
                    dve.wait_ge(Ehi, b)
                    gr = GROUPS - 1
                    lo(diagonal[:, 32 * gr:32 * gr + (CH - 1) * (P + 1) + 1:P + 1], Ef[:, :],
                       diagonal[:, 0:(CH - 1) * (P + 1) + 1:P + 1]).then_inc(Elo, 1)
                    dve.wait_ge(PWhi, b * 2 - 1)
                    lo(Pl[:, :, :].rearrange("p c n -> p (c n)"), Pf, Ph[:, :, :].rearrange("p c n -> p (c n)")).then_inc(Plo, 1)
                    dve.wait_ge(PWhi, b * 2)
                    third = Ws[64:96, :, :].rearrange("p c n -> p (c n)")
                    lo(third, Wf[64:96, :], third).then_inc(Wlo, 1)
                elif task[0] == "sums":
                    dve.wait_ge(sumhi, b * 2 - 1)
                    lo(Bs[32:64, :], bank[32:64, :], Bs[32:64, :]).then_inc(used, 1)
                elif task[0] == "sums1":
                    dve.wait_ge(sumhi, b * 2)
                    lo(B1s[32:64, :], bank[32:64, 0:2], B1s[32:64, :]).then_inc(used, 1)
                elif task[0] == "den":
                    nc.vector.tensor_tensor(rd[:, :], bank[:, 0:2 * CH].rearrange("p (c k) -> p c k", k=2)[:, :, 0],
                                            TM[:, CNT], ALU.mult).then_inc(used, 1)
                    wait_used(dve, kind, b, pos)
                    nc.vector.reciprocal(rd[:, :], rd[:, :]).then_inc(rd_done, 1)
                elif task[0] == "pool":
                    c = task[1]
                    wait(dve, out_put[c % 2], b * (16 * CH // 2) + 16 * (c // 2 - CH // 2))
                    if c == 0:
                        dve.wait_ge(rd_done, b)
                    nc.vector.scalar_tensor_tensor(oo[:, c % 2, :], bank[:, :], rd[:, c:c + 1], xnh[:, c, :].bitcast(f32),
                                                   ALU.mult, ALU.add).then_inc(used, 1)

            def link(ins, b, number):
                ins.then_inc(chain, 1)
                dve.wait_ge(chain, b * NCHAIN + (number - NCHAIN))

            def maxima(b):
                nc.vector.tensor_tensor_scan(G8[:, P - 1::-1], s8[:, P - 1::-1], s8[:, P - 1::-1], NEG, ALU.max, ALU.max
                                             ).then_inc(chain, 1)
                link(nc.vector.tensor_tensor_scan(F8[:, 1:P + 1], s8[:, :], s8[:, :], NEG, ALU.max, ALU.max), b, 2)
                nc.vector.tensor_scalar(DG[:, :], ident[0:CH, 0:CH], F8[:, P:P + 1], None, ALU.mult).then_inc(chain, 1)

            def row_maxima(b):
                nc.vector.tensor_tensor(Ef[:, :], st[:, 0:CH], st[:, CH:2 * CH], ALU.subtract).then_inc(chain, 1)
                link(nc.vector.tensor_tensor(t88[:, :], st[0:CH, CH:2 * CH], TM[0:CH, SEEN], ALU.add), b, 5)
                nc.vector.reduce_max(mc[:, :], t88[:, :], AX.X).then_inc(chain, 1)
                link(nc.vector.tensor_scalar(m0[:, :], s8[:, :], TM[0:CH, NC:NC + 1], None, ALU.add), b, 7)
                link(nc.vector.scalar_tensor_tensor(m0[:, :], G8[:, 1:P + 1], TM[0:CH, NP_:NP_ + 1], m0[:, :],
                                                    ALU.add, ALU.max), b, 8)
                link(nc.vector.scalar_tensor_tensor(m0[:, :], F8[:, 0:P], TM[0:CH, NS:NS + 1], m0[:, :],
                                                    ALU.add, ALU.max), b, 9)
                nc.vector.tensor_scalar(m8[:, :], m0[:, :], mc[:, :], -1.0, ALU.max, ALU.mult).then_inc(chain, 1)

            def part(kind, b):
                for t, s, row in BODIES[kind]:
                    for task, _, _ in row:
                        if task[0] == "bias":
                            dve.wait_ge(bias_turned, 1)
                            nc.vector.tensor_copy(bcol[:, :], yb[0][:, 0:NBR]).then_inc(bcol_done, 1)
                            dve.wait_ge(bcol_done, 1)
                            dve.wait_ge(const_done, 2)
                            diagonal = vz[:, :, :].rearrange("p c n -> p (c n)")
                            nc.vector.tensor_copy(diagonal[:, ::CH + 1], bcol[:, R_V:R_V + 1].to_broadcast([P, CH])
                                                  ).then_inc(vz_done, 1)
                    if kind != "tail":
                        S, ring = slot_no(b, t, s), s % 2
                        nxt = (s + 1) % HC
                        dve.wait_ge(w1hi, S + 2)
                        lo(w1l[:, nxt % 2, :], w1T[:, nxt, :], w1h[:, nxt % 2, :]).then_inc(w1lo, 1)
                        dve.wait_ge(hhi, S + 1)
                        lo(hl[:, ring, :], g[:, ring, :], hh[:, ring, :]).then_inc(hlo, 1)
                        if kind != "first" or t == 1:
                            split_w2(S, s)
                    for task, pos, _ in row:
                        task_part(kind, b, t, task, pos)
                    if kind == "first" and t == 0:
                        split_w2(S, s)

            def split_w2(S, s):
                dve.wait_ge(w2hi, S + 1)
                lo(w2l[:, s % 2, :], w2T[:, s, :], w2h[:, s % 2, :]).then_inc(w2lo, 1)

            for n, task in enumerate(PROLOGUE):
                task_part("first", 0, 0, task, n)
            dve.wait_ge(w1hi, 1)
            lo(w1l[:, 0, :], w1T[:, 0, :], w1h[:, 0, :]).then_inc(w1lo, 1)
            dve.wait_ge(W1hi, 1)
            lo(W1l[:, :, :].rearrange("p c a -> p (c a)"), x1T[:, 0, :], W1h[:, :, :].rearrange("p c a -> p (c a)")
               ).then_inc(W1lo, 1)
            run(dve, part)


_INS = ["x", "itok_B_0_15", "itok_B_0_2", "L0_cond_fc1_w", "L0_cond_fc1_b", "L0_cond_fc2_w", "L0_cond_fc2_b",
        "L0_cond_experts_w", "L0_cond_experts_b", "L1_cond_W1", "L1_cond_b1", "L1_cond_v"]


def kernel(**inputs):
    import numpy as np
    import concourse.bacc as bacc
    from concourse.bass_utils import run_bass_kernel_spmd

    nc = bacc.Bacc("TRN2", target_bir_lowering=False, num_devices=1)
    arrays, args = {}, []
    for name in _INS:
        a = np.ascontiguousarray(inputs[name])
        arrays[f"in_{name}"] = a
        args.append(nc.dram_tensor(f"in_{name}", a.shape, mybir.dt.from_np(a.dtype), kind="ExternalInput").ap())
    args.append(nc.dram_tensor("out_x", (NB, SEQ, D), mybir.dt.float32, kind="ExternalOutput").ap())
    build(nc, *args)
    r = run_bass_kernel_spmd(nc, [arrays], core_ids=[0])
    return r.results[0]["out_x"]
```

```python
import concourse.bass as bass
from concourse import mybir
from contextlib import ExitStack

NB, SEQ, D = 4, 1024, 512
HID, SHARED, PART = 2048, 384, 128
A = 128
P = 128
TT = 512
HC, DC, OC = HID // P, D // P, D // P
CH = SEQ // P
CT = TT // P
NEG = -1.0e30
GROUPS = 4
RAW = 4
OUTS = 4

TRI = slice(0, P)
CROSS = slice(P, P + CH)
SEEN = slice(P + CH, P + 2 * CH)
CNT = slice(P + 2 * CH, P + 3 * CH)
NS, NP_, NC = P + 3 * CH, P + 3 * CH + 1, P + 3 * CH + 2
MW = P + 3 * CH + 4

R_FC1, R_FC2, R_EXP, R_B1, R_V = 0, HC, HC + SHARED // P, HC + SHARED // P + NB, HC + SHARED // P + NB + 1
NBR = R_V + 1


BANK = {"x", "w1", "w2", "xn", "attn", "score", "stats", "bc", "sums", "sums1", "den", "pool"}
LOADED = {"x", "w1", "w2"}
PROLOGUE = [("x", 0, 0, 0), ("x", 0, 0, 1), ("w1", 0), ("x", 0, 0, 2), ("x", 0, 0, 3), ("w1", 1)]


def each(kind):
    return [(kind, oc) for oc in range(OC)]


def x1_tasks(s):
    return {0: ([], each("ysum")), 1: ([], each("x1")), 2: (each("x1lo"), [("xn", 0)]), 3: ([("xn", 1)], [("attn",)]),
            4: ([("xn", 2)], [("xn", 3)]), 5: ([("score",)], [])}.get(s, ([], []))


def pool_tasks(s):
    return {6: ([("stats",)], []), 8: ([("bc", 0)], [("bc", 1)]), 9: ([], [("expE",), ("expPW",)]),
            10: ([("sums",)], [("sums1",)]), 11: ([("den",)], []), 12: ([("pool", 0)], [("pool", 1)]),
            13: ([("pool", 2)], [("pool", 3)]), 14: ([("pool", 4)], [("pool", 5)]),
            15: ([("pool", 6)], [("pool", 7)])}.get(s, ([], []))


def load_tasks(kind, t, s):
    x_ = lambda c: ("x", t, 1 - t, c)
    if kind == "first" and t == 0:
        w1 = [("w1", s + 2)] if s + 2 < HC else []
        w2 = {0: [(0, 0), (1, 0), (2, 0), (3, 0)], 3: [(2, 1), (3, 1)]}.get(
            s, [((s - 1) % 4, 1)] if s < 3 else [(s % 4, s // 4 + 1)] if s < 12 else [])
        w2 = [("w2", ob, q, 0) for ob, q in w2]
        late = {12: [x_(0)], 13: [x_(1)], 14: [x_(2)], 15: [x_(3)]}.get(s, [])
        return w1 + w2[:len(w2) // 2], w2[len(w2) // 2:] + late
    if t == 0:
        ex = lambda q: ("w2", OC - 1, q, 0)
        return {2: ([ex(1)], []), 5: ([], [x_(0)]), 6: ([], [x_(1)]), 7: ([ex(2)], [x_(2)]), 9: ([x_(3)], []),
                11: ([], [ex(3)])}.get(s, ([], []))
    return {5: ([], [x_(0)]), 6: ([x_(1)], []), 8: ([x_(2)], []), 10: ([x_(3)], []),
            12: ([("w2", OC - 1, 0, 1)], [])}.get(s, ([], []))


def slot_tasks(kind, t, s):
    rows = [load_tasks(kind, t, s)]
    if t == 1 or kind == "loop":
        rows.append(x1_tasks(s))
    if t == 0 and kind == "loop":
        rows.append(pool_tasks(s))
    return sum((r[0] for r in rows), []), sum((r[1] for r in rows), [])


TAIL_ORDER = [("ysum", 0), ("ysum", 1), ("x1", 0), ("ysum", 2), ("x1", 1), ("x1lo", 0), ("ysum", 3), ("x1", 2),
              ("x1lo", 1), ("x1", 3), ("x1lo", 2), ("x1lo", 3), ("attn",), ("xn", 0), ("score",), ("xn", 1), ("stats",),
              ("expE",), ("xn", 2), ("xn", 3), ("sums",), ("sums1",), ("bc", 0), ("bc", 1), ("expPW",), ("den",)] + \
             [("pool", c) for c in range(CH)]


def body(kind):
    job = load = len(PROLOGUE) if kind == "first" else 0
    out = []
    for t, s in [(0, 0)] if kind == "tail" else [(t, s) for t in range(2) for s in range(HC)]:
        rows = []
        for part in ([], TAIL_ORDER) if kind == "tail" else slot_tasks(kind, t, s):
            rows.append([])
            for task in part:
                rows[-1].append((task, job, load))
                job += task[0] in BANK
                load += task[0] in LOADED
        out.append((t, s, *rows))
    return out, job, load


FIRST, J0, L0 = body("first")
LOOP, J, L = body("loop")
TAIL, _, _ = body("tail")
assert J % 2 == 0 and L % RAW == 0
BODIES = {"first": FIRST, "loop": LOOP, "tail": TAIL}


def job_of(kind, b, pos):
    return pos if kind == "first" else b * J + (J0 - J + pos)


def bank_of(kind, pos):
    return pos % 2 if kind == "first" else (J0 + pos) % 2


def bank_turn(kind, b, pos):
    return pos // 2 if kind == "first" else b * (J // 2) + ((J0 + pos) // 2 - J // 2)


def at(kind, t, task):
    return next(pos for tt, _, early, late in BODIES[kind] for k, pos, _ in early + late if tt == t and k == task)


def at_before(t, task):
    return at("loop", t, task) - J


def raw_of(kind, pos):
    return pos % RAW if kind == "first" else (L0 + pos) % RAW


def raw_turn(kind, b, pos):
    return pos // RAW if kind == "first" else b * (L // RAW) + ((L0 + pos) // RAW - L // RAW)


def build(nc, x, tok_e, tok_t, fc1_w, fc1_b, fc2_w, fc2_b, exp_w, exp_b, W1, b1, v, out):
    f32, f32r, i32 = mybir.dt.float32, mybir.dt.float32r, mybir.dt.int32
    ALU, ACT, AX = mybir.AluOpType, mybir.ActivationFunctionType, mybir.AxisListType

    ctx = ExitStack()
    with ctx:
        def sb(name, shape, dt=f32):
            return ctx.enter_context(nc.sbuf_tensor(name, shape, dt))

        def pb(name):
            return ctx.enter_context(nc.psum_tensor(name, [P, 512], f32))

        def sem(name):
            return ctx.enter_context(nc.semaphore(name))

        w1T = sb("w1T", [P, HC, D])
        w2T = sb("w2T", [P, HC, D])
        w1h, w1l = sb("w1h", [P, 2, D], f32r), sb("w1l", [P, 2, D], f32r)
        w2h, w2l = sb("w2h", [P, 2, D], f32r), sb("w2l", [P, 2, D], f32r)
        xh = [sb(f"xh{i}", [P, DC, TT], f32r) for i in range(2)]
        xl = [sb(f"xl{i}", [P, DC, TT], f32r) for i in range(2)]
        x1T = sb("x1T", [P, OC, TT])
        raw = sb("raw", [P, RAW, 512])
        g = sb("g", [P, 2, TT])
        hh, hl = sb("hh", [P, 2, TT], f32r), sb("hl", [P, 2, TT], f32r)
        xnh, xnl = sb("xnh", [P, CH, D], f32r), sb("xnl", [P, CH, D], f32r)
        W1h, W1l = sb("W1h", [P, DC, A], f32r), sb("W1l", [P, DC, A], f32r)
        Ph, Pl = sb("Ph", [P, CH, P], f32r), sb("Pl", [P, CH, P], f32r)
        Ws = sb("Ws", [P, CH, P], f32r)
        E4 = sb("E4", [P, CH, P], f32r)
        Bs = sb("Bs", [P, D], f32r)
        B1s = sb("B1s", [P, 2], f32r)
        th = sb("th", [P, TT])
        ident = sb("ident", [P, P])
        ones2 = sb("ones2", [P, 2], f32r)
        ones8 = sb("ones8", [CH, P])
        rep = sb("rep", [CH, GROUPS, 32])
        K0, KS, KP, KC = (sb(n, [P, MW]) for n in ("K0", "KS", "KP", "KC"))
        kt = sb("kt", [P, MW])
        TM = sb("TM", [P, MW])
        ty = sb("ty", [P, 1], i32)
        tyf = sb("tyf", [P, 4])
        cnti = sb("cnti", [P, 2 * CH], i32)
        brow = sb("brow", [NBR, P])
        bcol = sb("bcol", [P, NBR])
        vz = sb("vz", [P, CH, CH])
        s8a, s8 = sb("s8a", [CH, P]), sb("s8", [CH, P])
        F8, G8 = sb("F8", [CH, P + 1]), sb("G8", [CH, P + 1])
        DG = sb("DG", [CH, CH])
        st = sb("st", [P, 2 * CH + 1])
        t88, m0 = sb("t88", [CH, CH]), sb("m0", [CH, P])
        mc = sb("mc", [CH, 1])
        m8 = sb("m8", [CH, P])
        Ef = sb("Ef", [P, CH])
        rd = sb("rd", [P, CH])

        Pf = x1T[:, 0:2, :].rearrange("p a n -> p (a n)")
        oo = x1T
        Wf = x1T[:, 2:4, :].rearrange("p a n -> p (a n)")

        yb = [pb(f"y{i}") for i in range(OC)]
        hb = [pb(f"h{i}") for i in range(2)]
        jb = [pb(f"j{i}") for i in range(2)]

        raw_in = [sem(f"raw_in{i}") for i in range(RAW)]
        bias_in, W1_in, type_in = sem("bias_in"), sem("W1_in"), sem("type_in")
        out_put = [sem(f"out_put{i}") for i in range(OUTS)]
        const_done, mask_done = sem("const_done"), sem("mask_done")
        gstep = sem("gstep")
        bias_turned, bcol_done, vz_done = sem("bias_turned"), sem("bcol_done"), sem("vz_done")
        job_done = sem("job_done")
        bank_read = [sem(f"bank_read{i}") for i in range(2)]
        fc1_done, fc2_done = sem("fc1_done"), sem("fc2_done")
        w1hi, w1lo, w2hi, w2lo = sem("w1hi"), sem("w1lo"), sem("w2hi"), sem("w2lo")
        W1hi, W1lo = sem("W1hi"), sem("W1lo")
        gelu_done, hhi, hlo = sem("gelu_done"), sem("hhi"), sem("hlo")
        xhi, xnhi = sem("xhi"), sem("xnhi")
        ysum, x1_done, x1hi, x1lo = sem("ysum"), sem("x1_done"), sem("x1hi"), sem("x1lo")
        chain = sem("chain")
        exp_done = sem("exp_done")
        passed = sem("passed")
        Ehi, Elo = sem("Ehi"), sem("Elo")
        PWhi, Plo, Wlo = sem("PWhi"), sem("Plo"), sem("Wlo")
        sumhi = sem("sumhi")
        rd_done, row_sum = sem("rd_done"), sem("row_sum")

        NCHAIN, DIAG = 10, 3

        def wait(eng, s, value):
            if not (isinstance(value, int) and value <= 0):
                eng.wait_ge(s, value)

        def wait_used(eng, kind, b, pos):
            eng.wait_ge(bank_read[bank_of(kind, pos)], bank_turn(kind, b, pos) + 1)

        def gate(eng, s, value):
            wait(eng, s, value)
            eng.sem_inc(passed, 1)

        def run(eng, part):
            part("first", 0)
            with eng.Fori(1, NB) as b:
                part("loop", b)
            part("tail", NB)

        def slot_no(b, t, s):
            return b * 2 * HC + (t * HC + s)

        def tile_before(b, t):
            return b * 2 + (t - 1)

        def batch_of(ap, b):
            return ap[bass.ds(b, 1)]

        block = ctx.enter_context(nc.Block())

        @block.sync
        def _(sp):
            order = {k: [r[0] for _, _, early, late in BODIES[k] for r in early + late if r[0][0] in LOADED] for k in ("first", "loop")}
            order["first"] = PROLOGUE + order["first"]

            def source(task, b):
                if task[0] == "x":
                    _, ahead, t, c = task
                    rows = batch_of(x, (b + ahead) % NB)
                    return rows[:, t * TT + c * P:t * TT + (c + 1) * P, :].rearrange("o p n -> (o p) n")
                if task[0] == "w1":
                    return fc1_w[task[1] * P:(task[1] + 1) * P, :]
                _, ob, q, ahead = task
                if ob < OC - 1:
                    return fc2_w[ob * P:(ob + 1) * P, q * 512:(q + 1) * 512]
                e = sp.value_load(batch_of(tok_e, (b + ahead) % NB).rearrange("(o n) -> o n", o=1),
                                  min_val=0, max_val=exp_w.shape[0] - 1)
                return batch_of(exp_w, e)[:, :, q * 512:(q + 1) * 512].rearrange("o p n -> (o p) n")

            def load(kind, b, n):
                slot = raw_of(kind, n)
                sp.dma_start(raw[:, slot, :], source(order[kind][n], b)).then_inc(raw_in[slot], 16)

            def follow(kind, b, pos, n):
                gate(sp, job_done, job_of(kind, b, pos) + 1)
                if n + RAW < len(order[kind]):
                    load(kind, b, n + RAW)
                else:
                    load("loop", b + 1, n + RAW - len(order[kind]))

            def part(kind, b):
                if kind != "first":
                    gate(sp, mask_done, b - 1)
                    sp.dma_start(ty[:, :], batch_of(tok_t, b - 1).rearrange("(o n) -> o n", o=1).to_broadcast([P, 1])
                                 ).then_inc(type_in, 16)
                for t, s, early, late in BODIES[kind]:
                    for task, pos, n in early + late:
                        if task[0] in LOADED:
                            follow(kind, b, pos, n)
                        if task[0] == "pool":
                            c = task[1]
                            gate(sp, row_sum, b * CH + (c + 1 - CH))
                            sp.dma_start(batch_of(out, b - 1)[:, c * P:(c + 1) * P, :].rearrange("o p n -> (o p) n"),
                                         oo[:, c % OUTS, :]).then_inc(out_put[c % OUTS], 16)

            for n in range(RAW):
                load("first", 0, n)
            for n in range(len(PROLOGUE)):
                follow("first", 0, n, n)
                if n == 1:
                    sp.dma_start(x1T[:, 0, :].rearrange("p (c a) -> p c a", c=DC),
                                 W1.rearrange("(c p) a -> p c a", p=P)).then_inc(W1_in, 16)
            run(sp, part)
            for i in range(OUTS):
                sp.wait_ge(out_put[i], 16 * NB * CH // OUTS)
            for i in range(RAW):
                sp.wait_ge(raw_in[i], 16 * len([n for n in range(L0 + (NB - 1) * L + RAW) if n % RAW == i]))

        @block.gpsimd
        def _(pool):
            steps = [0]

            def link(ins):
                steps[0] += 1
                ins.then_inc(gstep, 1)
                pool.wait_ge(gstep, steps[0])

            def mark(ap, coef, count, cm, base=0, equal=False, fill=NEG):
                k = 1 if equal else -1
                return nc.gpsimd.affine_select(
                    out=ap, in_=ap, compare_op=ALU.not_equal if equal else ALU.is_ge, fill=fill,
                    base=k * base, pattern=[[k * coef, count]], channel_multiplier=k * cm)

            link(nc.gpsimd.memset(ident[:, :], 0.0))
            mark(ident[:, :], -1, P, 1, equal=True, fill=1.0).then_inc(const_done, 1)
            pool.wait_ge(const_done, 1)
            for r, src in ((R_FC1, fc1_b), (R_FC2, fc2_b), (R_B1, b1), (R_V, v)):
                pool.dma_start(brow[r:r + src.shape[0] // P, :], src.rearrange("(c p) -> c p", p=P)).then_inc(bias_in, 16)
            for b in range(NB):
                e = pool.value_load(tok_e[b:b + 1].rearrange("(o n) -> o n", o=1), min_val=0, max_val=exp_b.shape[0] - 1)
                pool.dma_start(brow[R_EXP + b:R_EXP + b + 1, :], batch_of(exp_b, e)).then_inc(bias_in, 16)
            link(nc.gpsimd.memset(ones8[:, :], 1.0))
            link(nc.gpsimd.memset(ones2[:, :].bitcast(f32), 1.0))
            link(nc.gpsimd.memset(vz[:, :, :], 0.0))
            link(nc.gpsimd.memset(E4[:, :, :].bitcast(f32), 0.0))
            link(nc.gpsimd.memset(F8[:, :], NEG))
            link(nc.gpsimd.memset(G8[:, :], NEG))
            for tile in (K0, KS, KP):
                link(nc.gpsimd.memset(tile[:, :], 0.0))
            link(nc.gpsimd.memset(KC[:, :], 0.0))
            for gr in range(GROUPS):
                link(nc.gpsimd.tensor_copy(rep[:, gr, :], ident[0:CH, 0:32]))
            link(mark(KS[:, TRI], 1, P, -1))
            link(mark(KP[:, TRI], -1, P, 1))
            link(mark(KC[:, TRI], -1, P, 1, equal=True))
            for gr in range(GROUPS):
                rows = slice(32 * gr, 32 * gr + 32)
                link(mark(KS[rows, CROSS], 1, CH, -1))
                link(mark(KP[rows, CROSS], -1, CH, 1))
                link(mark(K0[rows, CROSS], -1, CH, 1, equal=True))
                link(mark(K0[rows, CROSS], 0, CH, 1, base=1 - CH))
            link(mark(KS[:, SEEN], -1, CH, 1))
            link(mark(KP[:, SEEN], 1, CH, -1))
            link(mark(K0[:, SEEN], -1, CH, 1, equal=True))
            link(nc.gpsimd.memset(KS[:, NS:NS + 1], NEG))
            link(nc.gpsimd.memset(KP[:, NP_:NP_ + 1], NEG))
            link(nc.gpsimd.memset(KC[:, NC:NC + 1], NEG))
            link(nc.gpsimd.memset(KC[:, CNT], float(SEQ - 1)))
            link(nc.gpsimd.iota(cnti[:, 0:CH], pattern=[[-P, CH]], base=SEQ, channel_multiplier=-1))
            link(nc.gpsimd.iota(cnti[:, CH:2 * CH], pattern=[[P, CH]], base=1, channel_multiplier=1))
            link(nc.gpsimd.tensor_copy(KS[:, CNT], cnti[:, 0:CH]))
            link(nc.gpsimd.tensor_copy(KP[:, CNT], cnti[:, CH:2 * CH]))
            nc.gpsimd.memset(kt[:, 0:1], 0.0).then_inc(const_done, 1)
            before_masks, per_mask = steps[0], 10

            def part(kind, b):
                if kind == "first":
                    return
                made = [0]

                def then(ins):
                    made[0] += 1
                    ins.then_inc(gstep, 1)
                    gate(pool, gstep, b * per_mask + (before_masks - per_mask + made[0]))

                pool.wait_ge(type_in, b * 16)
                gate(pool, rd_done, b - 1)
                then(nc.gpsimd.tensor_copy(tyf[:, 0:1], ty[:, :]))
                then(nc.gpsimd.tensor_scalar(tyf[:, 1:2], tyf[:, 0:1], 0.0, None, ALU.is_equal))
                then(nc.gpsimd.tensor_scalar(tyf[:, 2:3], tyf[:, 0:1], 1.0, None, ALU.is_equal))
                then(nc.gpsimd.tensor_tensor(tyf[:, 3:4], tyf[:, 1:2], tyf[:, 2:3], ALU.add))
                then(nc.gpsimd.tensor_scalar(tyf[:, 3:4], tyf[:, 3:4], -1.0, 1.0, ALU.mult, ALU.add))
                then(nc.gpsimd.tensor_scalar(kt[:, :], KS[:, :], tyf[:, 2:3], None, ALU.mult))
                then(nc.gpsimd.tensor_scalar(TM[:, :], KP[:, :], tyf[:, 1:2], None, ALU.mult))
                then(nc.gpsimd.tensor_tensor(TM[:, :], TM[:, :], kt[:, :], ALU.add))
                then(nc.gpsimd.tensor_scalar(kt[:, :], KC[:, :], tyf[:, 3:4], None, ALU.mult))
                then(nc.gpsimd.tensor_tensor(TM[:, :], TM[:, :], kt[:, :], ALU.add))
                nc.gpsimd.tensor_tensor(TM[:, :], TM[:, :], K0[:, :], ALU.add).then_inc(mask_done, 1)
                for t, s, early, late in BODIES[kind]:
                    for task, pos, _ in early + late:
                        if task[0] == "pool":
                            c = task[1]
                            wait_used(pool, kind, b, pos)
                            nc.gpsimd.tensor_tensor(oo[:, c % OUTS, :], oo[:, c % OUTS, :], xnl[:, c, :].bitcast(f32),
                                                    ALU.add).then_inc(row_sum, 1)

            run(pool, part)

        @block.tensor
        def _(pe):
            def three(ps, ah, al, bh, bl, first, last):
                nc.tensor.matmul(ps, ah, bh, start=first, stop=False)
                nc.tensor.matmul(ps, ah, bl, start=False, stop=False)
                return nc.tensor.matmul(ps, al, bh, start=False, stop=last)

            def fc1(kind, b, t, s):
                ring, S = s % 2, slot_no(b, t, s)
                if s == 0:
                    last_chunk = (at(kind, 0, ("x", 0, 1, CT - 1)) if t == 1 else
                                  PROLOGUE.index(("x", 0, 0, CT - 1)) if kind == "first" else at_before(1, ("x", 1, 0, CT - 1)))
                    wait_used(pe, kind, b, last_chunk)
                pe.wait_ge(w1lo, S + 1)
                wait(pe, gelu_done, S - 1)
                for dc in range(DC):
                    w = slice(dc * P, (dc + 1) * P)
                    last = three(hb[ring][:, :], w1h[:, ring, w], w1l[:, ring, w], xh[t][:, dc, :], xl[t][:, dc, :],
                                 dc == 0, dc == DC - 1)
                last.then_inc(fc1_done, 1)

            def fc2(b, t, s):
                ring, S = s % 2, slot_no(b, t, s)
                pe.wait_ge(w2lo, S + 1)
                pe.wait_ge(hlo, S + 1)
                for oc in range(OC):
                    if s == 0:
                        wait(pe, ysum, tile_before(b, t) * OC + (oc + 1))
                    w = slice(oc * P, (oc + 1) * P)
                    three(yb[oc][:, :], w2h[:, ring, w], w2l[:, ring, w], hh[:, ring, :], hl[:, ring, :],
                          s == 0, s == HC - 1).then_inc(fc2_done, 1)

            def job(kind, b, t, task, pos, n):
                if task[0] not in BANK:
                    return
                bank = jb[bank_of(kind, pos)]
                T1 = tile_before(b, t)
                wait(pe, bank_read[bank_of(kind, pos)], bank_turn(kind, b, pos))
                if task[0] in LOADED:
                    r = raw_of(kind, n)
                    pe.wait_ge(raw_in[r], raw_turn(kind, b, n) * 16 + 16)
                    for i in range(4):
                        last = nc.tensor.transpose(bank[:, i * P:(i + 1) * P], raw[:, r, i * P:(i + 1) * P], ident[:, :])
                elif task[0] == "xn":
                    c = task[1]
                    pe.wait_ge(x1_done, T1 * OC + OC)
                    for i in range(OC):
                        last = nc.tensor.transpose(bank[:, i * P:(i + 1) * P], x1T[:, i, c * P:(c + 1) * P], ident[:, :])
                elif task[0] == "attn":
                    if kind == "first":
                        pe.wait_ge(W1lo, 1)
                    for dc in range(DC):
                        pe.wait_ge(x1lo, T1 * OC + (dc + 1))
                        last = three(bank[:, :], W1h[:, dc, :], W1l[:, dc, :], xh[1 - t][:, dc, :], xl[1 - t][:, dc, :],
                                     dc == 0, dc == DC - 1)
                elif task[0] == "score":
                    wait_used(pe, kind, b, at(kind, t, ("attn",)))
                    if kind == "first":
                        pe.wait_ge(vz_done, 1)
                    for i in range(CT):
                        last = nc.tensor.matmul(bank[0:CH, 0:P], vz[:, (1 - t) * CT + i, :], th[:, i * P:(i + 1) * P],
                                                start=(i == 0), stop=(i == CT - 1))
                elif task[0] == "stats":
                    pe.wait_ge(chain, b * NCHAIN + (DIAG - NCHAIN))
                    nc.tensor.matmul(bank[:, CH:2 * CH], ones8[:, :], DG[:, :], start=True, stop=True)
                    nc.tensor.transpose(bank[:, 0:CH], s8[:, :], ident[0:CH, 0:CH])
                    last = nc.tensor.matmul(bank[:, 2 * CH:2 * CH + 1], rep[:, :, :].rearrange("c g k -> c (g k)"),
                                            F8[:, P:P + 1], start=True, stop=True)
                elif task[0] == "bc":
                    pe.wait_ge(chain, b * NCHAIN)
                    for i in range(CT):
                        c = task[1] * CT + i
                        last = nc.tensor.matmul(bank[:, i * P:(i + 1) * P], ident[0:CH, c:c + 1].to_broadcast([CH, P]),
                                                m8[:, :], start=True, stop=True)
                elif task[0] == "sums":
                    pe.wait_ge(Elo, b)
                    wait_used(pe, kind, b, at(kind, t, ("xn", CT - 1)))
                    for c in range(CH):
                        nc.tensor.matmul(bank[:, :], E4[:, c, :], xnh[:, c, :], start=(c == 0), stop=False)
                        last = nc.tensor.matmul(bank[:, :], E4[:, c, :], xnl[:, c, :], start=False, stop=(c == CH - 1))
                elif task[0] == "sums1":
                    for c in range(CH):
                        last = nc.tensor.matmul(bank[:, 0:2], E4[:, c, :], ones2[:, :], start=(c == 0), stop=(c == CH - 1))
                elif task[0] == "den":
                    pe.wait_ge(Plo, b)
                    pe.wait_ge(Wlo, b)
                    wait_used(pe, kind, b, at(kind, t, ("sums1",)))
                    for c in range(CH):
                        two = bank[:, 2 * c:2 * c + 2]
                        nc.tensor.matmul(two, Ph[:, c, :], ones2[:, :], start=True, stop=False)
                        nc.tensor.matmul(two, Pl[:, c, :], ones2[:, :], start=False, stop=False)
                        last = nc.tensor.matmul(two, Ws[:, c, :], B1s[:, :], start=False, stop=True)
                elif task[0] == "pool":
                    c = task[1]
                    three(bank[:, :], Ph[:, c, :], Pl[:, c, :], xnh[:, c, :], xnl[:, c, :], True, False)
                    last = nc.tensor.matmul(bank[:, :], Ws[:, c, :], Bs[:, :], start=False, stop=True)
                last.then_inc(job_done, 1)

            def part(kind, b):
                for t, s, early, late in BODIES[kind]:
                    if kind != "tail":
                        fc1(kind, b, t, s)
                    if kind == "first" and t == 0 and s == 0:
                        pe.wait_ge(bias_in, 16 * (4 + NB))
                        nc.tensor.transpose(yb[0][:, 0:NBR], brow[:, :], ident[0:NBR, 0:NBR]).then_inc(bias_turned, 1)
                    for task, pos, n in early:
                        job(kind, b, t, task, pos, n)
                    if s > 0:
                        fc2(b, t, s - 1)
                    elif t == 1:
                        fc2(b, 0, HC - 1)
                    elif kind != "first":
                        fc2(b - 1, 1, HC - 1)
                    for task, pos, n in late:
                        job(kind, b, t, task, pos, n)

            pe.wait_ge(const_done, 1)
            for n, task in enumerate(PROLOGUE):
                job("first", 0, 0, task, n, n)
            run(pe, part)

        @block.scalar
        def _(act):
            def hi(out_, in_):
                return nc.scalar.activation(out_, in_, ACT.Copy)

            def split_w1(kind, b, t, s):
                nxt, S1 = (s + 1) % HC, slot_no(b, t, s + 1)
                if kind == "first" and t == 0 and nxt:
                    wait_used(act, kind, b, PROLOGUE.index(("w1", nxt)) if nxt < 2 else at(kind, 0, ("w1", nxt)))
                wait(act, fc1_done, S1 - 1)
                hi(w1h[:, nxt % 2, :], w1T[:, nxt, :]).then_inc(w1hi, 1)

            def split_w2(kind, b, t, s):
                if t == 0 and s % 4 == 0:
                    if kind == "loop" and s == 0:
                        wait_used(act, kind, b, at_before(1, ("w2", OC - 1, 0, 1)))
                    else:
                        wait_used(act, kind, b, at(kind, 0, ("w2", OC - 1, s // 4, 0)))
                wait(act, fc2_done, (slot_no(b, t, s) - 2) * OC + OC)
                hi(w2h[:, s % 2, :], w2T[:, s, :]).then_inc(w2hi, 1)

            def task_part(kind, b, t, task, pos):
                T1 = tile_before(b, t)
                bank = jb[bank_of(kind, pos)]
                if task[0] in ("x", "xn", "attn", "sums", "sums1"):
                    act.wait_ge(job_done, job_of(kind, b, pos) + 1)
                if task[0] == "x":
                    _, _, tt, c = task
                    hi(xh[tt][:, :, c * P:(c + 1) * P], bank[:, :].rearrange("p (d n) -> p d n", d=DC)).then_inc(xhi, 1)
                elif task[0] == "x1":
                    oc = task[1]
                    act.wait_ge(x1_done, T1 * OC + (oc + 1))
                    hi(xh[1 - t][:, oc, :], x1T[:, oc, :]).then_inc(x1hi, 1)
                elif task[0] == "xn":
                    if task[1] == 0 and t == 1 and kind == "loop":
                        wait_used(act, kind, b, at(kind, 0, ("pool", CH - 1)))
                    hi(xnh[:, (1 - t) * CT + task[1], :], bank[:, :]).then_inc(xnhi, 1)
                elif task[0] == "attn":
                    nc.scalar.activation(th[:, :], bank[:, :], ACT.Tanh, bias=bcol[:, R_B1:R_B1 + 1]
                                         ).then_inc(bank_read[bank_of(kind, pos)], 1)
                elif task[0] == "expE":
                    act.wait_ge(chain, b * NCHAIN + (DIAG + 1 - NCHAIN))
                    nc.scalar.activation(Ef[:, :], Ef[:, :], ACT.Exp).then_inc(exp_done, 1)
                elif task[0] == "expPW":
                    wait_used(act, kind, b, at(kind, t, ("bc", 1)))
                    for tile in (Pf, Wf):
                        nc.scalar.activation(tile, tile, ACT.Exp).then_inc(exp_done, 1)
                    for i, (part_, full) in enumerate(((Ph, Pf), (Ws, Wf))):
                        act.wait_ge(exp_done, b * 3 - 1 + i)
                        hi(part_[:, :, :].rearrange("p c n -> p (c n)"), full).then_inc(PWhi, 1)
                elif task[0] == "sums":
                    hi(Bs[:, :], bank[:, :]).then_inc(sumhi, 1)
                elif task[0] == "sums1":
                    hi(B1s[:, :], bank[:, 0:2]).then_inc(sumhi, 1)

            def part(kind, b):
                for t, s, early, late in BODIES[kind]:
                    if kind != "tail":
                        S, ring = slot_no(b, t, s), s % 2
                        split_w1(kind, b, t, s)
                        act.wait_ge(fc1_done, S + 1)
                        wait(act, hlo, S - 1)
                        if kind == "first" and t == 0 and s == 0:
                            act.wait_ge(bcol_done, 1)
                        nc.scalar.activation(g[:, ring, :], hb[ring][:, :], ACT.Gelu,
                                             bias=bcol[:, R_FC1 + s:R_FC1 + s + 1]).then_inc(gelu_done, 1)
                        wait(act, fc2_done, (S - 2) * OC + OC)
                        act.wait_ge(gelu_done, S + 1)
                        hi(hh[:, ring, :], g[:, ring, :]).then_inc(hhi, 1)
                        if kind != "first" or t == 1:
                            split_w2(kind, b, t, s)
                    for task, pos, _ in early + late:
                        task_part(kind, b, t, task, pos)
                    if kind == "first" and t == 0:
                        split_w2(kind, b, t, s)

            for n, task in enumerate(PROLOGUE):
                task_part("first", 0, 0, task, n)
            wait_used(act, "first", 0, PROLOGUE.index(("w1", 0)))
            hi(w1h[:, 0, :], w1T[:, 0, :]).then_inc(w1hi, 1)
            act.wait_ge(W1_in, 16)
            hi(W1h[:, :, :].rearrange("p c a -> p (c a)"), x1T[:, 0, :]).then_inc(W1hi, 1)
            run(act, part)

        @block.vector
        def _(dve):
            def lo(out_, in_, hi_):
                return nc.vector.tensor_tensor(out_, in_, hi_.bitcast(f32), ALU.subtract)

            def task_part(kind, b, t, task, pos):
                T1 = tile_before(b, t)
                bk = bank_of(kind, pos)
                bank, used = jb[bk], bank_read[bk]
                if task[0] in ("w1", "w2", "score", "stats", "bc", "den", "pool"):
                    dve.wait_ge(job_done, job_of(kind, b, pos) + 1)
                if task[0] == "x":
                    _, _, tt, c = task
                    in_prologue = kind == "first" and pos < len(PROLOGUE)
                    dve.wait_ge(xhi, c + 1 if in_prologue else b * 2 * CT + ((t + 1) * CT + c + 1))
                    where = (slice(None), slice(None), slice(c * P, (c + 1) * P))
                    lo(xl[tt][where], bank[:, :].rearrange("p (d n) -> p d n", d=DC), xh[tt][where]).then_inc(used, 1)
                elif task[0] == "w1":
                    nc.vector.tensor_copy(w1T[:, task[1], :], bank[:, :]).then_inc(used, 1)
                elif task[0] == "w2":
                    _, ob, q, _ = task
                    nc.vector.tensor_copy(w2T[:, 4 * q:4 * q + 4, ob * P:(ob + 1) * P],
                                          bank[:, :].rearrange("p (d n) -> p d n", d=4)).then_inc(used, 1)
                elif task[0] == "ysum":
                    oc = task[1]
                    bias = (bcol[:, R_FC2 + oc:R_FC2 + oc + 1] if oc < OC - 1 else
                            bcol[:, bass.ds(b + (R_EXP + t - 1), 1)])
                    if t == 1 and kind == "loop":
                        dve.wait_ge(out_put[oc], b * (16 * CH // OUTS))
                    dve.wait_ge(fc2_done, T1 * HC * OC + ((HC - 1) * OC + oc + 1))
                    nc.vector.scalar_tensor_tensor(x1T[:, oc, :], yb[oc][:, :], bias, xh[1 - t][:, oc, :].bitcast(f32),
                                                   ALU.add, ALU.add).then_inc(ysum, 1)
                elif task[0] == "x1":
                    oc = task[1]
                    dve.wait_ge(ysum, T1 * OC + (oc + 1))
                    nc.vector.tensor_tensor(x1T[:, oc, :], x1T[:, oc, :], xl[1 - t][:, oc, :].bitcast(f32),
                                            ALU.add).then_inc(x1_done, 1)
                elif task[0] == "x1lo":
                    oc = task[1]
                    dve.wait_ge(x1hi, T1 * OC + (oc + 1))
                    lo(xl[1 - t][:, oc, :], x1T[:, oc, :], xh[1 - t][:, oc, :]).then_inc(x1lo, 1)
                elif task[0] == "xn":
                    c = (1 - t) * CT + task[1]
                    dve.wait_ge(xnhi, T1 * CT + (task[1] + 1))
                    if task[1] == 0 and t == 1 and kind == "loop":
                        dve.wait_ge(row_sum, b * CH)
                    lo(xnl[:, c, :], bank[:, :], xnh[:, c, :]).then_inc(used, 1)
                elif task[0] == "score":
                    if t == 1:
                        nc.vector.tensor_copy(s8a[:, :], bank[0:CH, 0:P]).then_inc(used, 1)
                    else:
                        nc.vector.tensor_tensor(s8[:, :], bank[0:CH, 0:P], s8a[:, :], ALU.add).then_inc(used, 1)
                        wait_used(dve, kind, b, pos)
                        maxima(b)
                elif task[0] == "stats":
                    nc.vector.tensor_copy(st[:, :], bank[:, 0:2 * CH + 1]).then_inc(used, 1)
                    dve.wait_ge(mask_done, b)
                    wait_used(dve, kind, b, pos)
                    row_maxima(b)
                elif task[0] == "bc":
                    for i in range(CT):
                        c = task[1] * CT + i
                        nc.vector.scalar_tensor_tensor(Pf[:, c * P:(c + 1) * P], bank[:, i * P:(i + 1) * P], st[:, c:c + 1],
                                                       TM[:, TRI], ALU.add, ALU.add)
                    half = slice(task[1] * TT, (task[1] + 1) * TT)
                    cross = TM[:, P + task[1] * CT:P + (task[1] + 1) * CT]
                    nc.vector.scalar_tensor_tensor(
                        Wf[:, half].rearrange("p (c n) -> p c n", c=CT), bank[:, :].rearrange("p (c n) -> p c n", c=CT),
                        st[:, 2 * CH:2 * CH + 1], cross.unsqueeze(2).to_broadcast([P, CT, P]), ALU.add, ALU.add
                    ).then_inc(used, 1)
                elif task[0] == "expE":
                    diagonal = E4[:, :, :].rearrange("p c n -> p (c n)")
                    dve.wait_ge(exp_done, b * 3 - 2)
                    for gr in range(GROUPS - 1):
                        last = nc.vector.tensor_copy(diagonal[:, 32 * gr:32 * gr + (CH - 1) * (P + 1) + 1:P + 1], Ef[:, :])
                    last.then_inc(Ehi, 1)
                    dve.wait_ge(Ehi, b)
                    gr = GROUPS - 1
                    lo(diagonal[:, 32 * gr:32 * gr + (CH - 1) * (P + 1) + 1:P + 1], Ef[:, :],
                       diagonal[:, 0:(CH - 1) * (P + 1) + 1:P + 1]).then_inc(Elo, 1)
                elif task[0] == "expPW":
                    dve.wait_ge(PWhi, b * 2 - 1)
                    lo(Pl[:, :, :].rearrange("p c n -> p (c n)"), Pf, Ph[:, :, :].rearrange("p c n -> p (c n)")).then_inc(Plo, 1)
                    dve.wait_ge(PWhi, b * 2)
                    third = Ws[64:96, :, :].rearrange("p c n -> p (c n)")
                    lo(third, Wf[64:96, :], third).then_inc(Wlo, 1)
                elif task[0] == "sums":
                    dve.wait_ge(sumhi, b * 2 - 1)
                    lo(Bs[32:64, :], bank[32:64, :], Bs[32:64, :]).then_inc(used, 1)
                elif task[0] == "sums1":
                    dve.wait_ge(sumhi, b * 2)
                    lo(B1s[32:64, :], bank[32:64, 0:2], B1s[32:64, :]).then_inc(used, 1)
                elif task[0] == "den":
                    nc.vector.tensor_tensor(rd[:, :], bank[:, 0:2 * CH].rearrange("p (c k) -> p c k", k=2)[:, :, 0],
                                            TM[:, CNT], ALU.mult).then_inc(used, 1)
                    wait_used(dve, kind, b, pos)
                    nc.vector.reciprocal(rd[:, :], rd[:, :]).then_inc(rd_done, 1)
                elif task[0] == "pool":
                    c = task[1]
                    if c >= OUTS:
                        dve.wait_ge(out_put[c % OUTS], b * (16 * CH // OUTS) + 16 * (c // OUTS - CH // OUTS))
                    if c == 0:
                        dve.wait_ge(rd_done, b)
                    nc.vector.scalar_tensor_tensor(oo[:, c % OUTS, :], bank[:, :], rd[:, c:c + 1], xnh[:, c, :].bitcast(f32),
                                                   ALU.mult, ALU.add).then_inc(used, 1)

            def link(ins, b, number):
                ins.then_inc(chain, 1)
                dve.wait_ge(chain, b * NCHAIN + (number - NCHAIN))

            def maxima(b):
                nc.vector.tensor_tensor_scan(G8[:, P - 1::-1], s8[:, P - 1::-1], s8[:, P - 1::-1], NEG, ALU.max, ALU.max
                                             ).then_inc(chain, 1)
                link(nc.vector.tensor_tensor_scan(F8[:, 1:P + 1], s8[:, :], s8[:, :], NEG, ALU.max, ALU.max), b, 2)
                nc.vector.tensor_scalar(DG[:, :], ident[0:CH, 0:CH], F8[:, P:P + 1], None, ALU.mult).then_inc(chain, 1)

            def row_maxima(b):
                nc.vector.tensor_tensor(Ef[:, :], st[:, 0:CH], st[:, CH:2 * CH], ALU.subtract).then_inc(chain, 1)
                link(nc.vector.tensor_tensor(t88[:, :], st[0:CH, CH:2 * CH], TM[0:CH, SEEN], ALU.add), b, 5)
                nc.vector.reduce_max(mc[:, :], t88[:, :], AX.X).then_inc(chain, 1)
                link(nc.vector.tensor_scalar(m0[:, :], s8[:, :], TM[0:CH, NC:NC + 1], None, ALU.add), b, 7)
                link(nc.vector.scalar_tensor_tensor(m0[:, :], G8[:, 1:P + 1], TM[0:CH, NP_:NP_ + 1], m0[:, :],
                                                    ALU.add, ALU.max), b, 8)
                link(nc.vector.scalar_tensor_tensor(m0[:, :], F8[:, 0:P], TM[0:CH, NS:NS + 1], m0[:, :],
                                                    ALU.add, ALU.max), b, 9)
                nc.vector.tensor_scalar(m8[:, :], m0[:, :], mc[:, :], -1.0, ALU.max, ALU.mult).then_inc(chain, 1)

            def part(kind, b):
                for t, s, early, late in BODIES[kind]:
                    if kind == "first" and t == 0 and s == 0:
                        dve.wait_ge(bias_turned, 1)
                        nc.vector.tensor_copy(bcol[:, :], yb[0][:, 0:NBR]).then_inc(bcol_done, 1)
                    if kind == "first" and t == 1 and s == 0:
                        dve.wait_ge(const_done, 2)
                        diagonal = vz[:, :, :].rearrange("p c n -> p (c n)")
                        nc.vector.tensor_copy(diagonal[:, ::CH + 1], bcol[:, R_V:R_V + 1].to_broadcast([P, CH])
                                              ).then_inc(vz_done, 1)
                    if kind != "tail":
                        S, ring = slot_no(b, t, s), s % 2
                        nxt = (s + 1) % HC
                        dve.wait_ge(w1hi, S + 2)
                        lo(w1l[:, nxt % 2, :], w1T[:, nxt, :], w1h[:, nxt % 2, :]).then_inc(w1lo, 1)
                        dve.wait_ge(hhi, S + 1)
                        lo(hl[:, ring, :], g[:, ring, :], hh[:, ring, :]).then_inc(hlo, 1)
                        if kind != "first" or t == 1:
                            split_w2(S, s)
                    for task, pos, _ in early + late:
                        task_part(kind, b, t, task, pos)
                    if kind == "first" and t == 0:
                        split_w2(S, s)

            def split_w2(S, s):
                dve.wait_ge(w2hi, S + 1)
                lo(w2l[:, s % 2, :], w2T[:, s, :], w2h[:, s % 2, :]).then_inc(w2lo, 1)

            for n, task in enumerate(PROLOGUE):
                task_part("first", 0, 0, task, n)
            dve.wait_ge(w1hi, 1)
            lo(w1l[:, 0, :], w1T[:, 0, :], w1h[:, 0, :]).then_inc(w1lo, 1)
            dve.wait_ge(W1hi, 1)
            lo(W1l[:, :, :].rearrange("p c a -> p (c a)"), x1T[:, 0, :], W1h[:, :, :].rearrange("p c a -> p (c a)")
               ).then_inc(W1lo, 1)
            run(dve, part)


_INS = ["x", "itok_B_0_15", "itok_B_0_2", "L0_cond_fc1_w", "L0_cond_fc1_b", "L0_cond_fc2_w", "L0_cond_fc2_b",
        "L0_cond_experts_w", "L0_cond_experts_b", "L1_cond_W1", "L1_cond_b1", "L1_cond_v"]


def kernel(**inputs):
    import numpy as np
    import concourse.bacc as bacc
    from concourse.bass_utils import run_bass_kernel_spmd

    nc = bacc.Bacc("TRN2", target_bir_lowering=False, num_devices=1)
    arrays, args = {}, []
    for name in _INS:
        a = np.ascontiguousarray(inputs[name])
        arrays[f"in_{name}"] = a
        args.append(nc.dram_tensor(f"in_{name}", a.shape, mybir.dt.from_np(a.dtype), kind="ExternalInput").ap())
    args.append(nc.dram_tensor("out_x", (NB, SEQ, D), mybir.dt.float32, kind="ExternalOutput").ap())
    build(nc, *args)
    r = run_bass_kernel_spmd(nc, [arrays], core_ids=[0])
    return r.results[0]["out_x"]
```

```python
import concourse.bass as bass
from concourse import mybir
from contextlib import ExitStack

NB, SEQ, D = 4, 1024, 512
HID, SHARED, PART = 2048, 384, 128
A = 128
P = 128
TT = 512
HC, DC, OC = HID // P, D // P, D // P
CH = SEQ // P
CT = TT // P
NEG = -1.0e30
GROUPS = 4
OUTS = 4
BC = CH // 2

TRI = slice(0, P)
CROSS = slice(P, P + CH)
SEEN = slice(P + CH, P + 2 * CH)
CNT = slice(P + 2 * CH, P + 3 * CH)
NS, NP_, NC = P + 3 * CH, P + 3 * CH + 1, P + 3 * CH + 2
MW = P + 3 * CH + 4

R_FC1, R_FC2, R_B1, R_V, R_EXP = 0, HC, HC + SHARED // P, HC + SHARED // P + 1, HC + SHARED // P + 2
NFIX, NBR = R_EXP, R_EXP + NB

W1_LOADS = [(0, 1), (1, 2), (2, 4), (4, 8), (8, 12), (12, 16)]

BANK = {"xn", "attn", "score", "stats", "bc", "sums", "sums1", "den", "pool"}


def each(kind):
    return [(kind, oc) for oc in range(OC)]


def x1_tasks(s):
    return {0: ([], each("ysum")), 1: ([], each("x1")), 2: (each("x1lo"), [("xn", 0)]), 3: ([("xn", 1)], [("attn",)]),
            4: ([("xn", 2)], [("xn", 3)]), 5: ([("score",)], [])}.get(s, ([], []))


def pool_tasks(s):
    return {6: ([("stats",)], []), 8: ([("bc", 0)], [("bc", 1)]), 9: ([], [("expE",), ("expPW", 0)]),
            10: ([("sums",), ("expPW", 1)], [("sums1",)]), 11: ([("den", 0, CH)], []),
            12: ([("pool", 0)], [("pool", 1)]), 13: ([("pool", 2)], [("pool", 3)]), 14: ([("pool", 4)], [("pool", 5)]),
            15: ([("pool", 6)], [("pool", 7)])}.get(s, ([], []))


def load_tasks(kind, t, s):
    return {5: ([], [("x", 0)]), 6: ([], [("x", 1)]), 7: ([("x", 2)], [("x", 3)])}.get(s, ([], []))


def slot_tasks(kind, t, s):
    rows = [load_tasks(kind, t, s)]
    if t == 1 or kind == "loop":
        rows.append(x1_tasks(s))
    if t == 0 and kind == "loop":
        rows.append(pool_tasks(s))
    return sum((r[0] for r in rows), []), sum((r[1] for r in rows), [])


TAIL_ORDER = [("ysum", 0), ("ysum", 1), ("x1", 0), ("ysum", 2), ("x1", 1), ("x1lo", 0), ("ysum", 3), ("x1", 2),
              ("x1lo", 1), ("x1", 3), ("x1lo", 2), ("x1lo", 3), ("attn",), ("xn", 0), ("score",), ("xn", 1), ("stats",),
              ("expE",), ("xn", 2), ("xn", 3), ("bc", 0), ("bc", 1), ("sums",), ("sums1",), ("expPW", 0), ("expPW", 1),
              ("den", 0, BC)] + [("pool", c) for c in range(BC)] + [("den", BC, CH)] + [("pool", c) for c in range(BC, CH)]


def body(kind):
    job = 0
    out = []
    for t, s in [(0, 0)] if kind == "tail" else [(t, s) for t in range(2) for s in range(HC)]:
        rows = []
        for part in ([], TAIL_ORDER) if kind == "tail" else slot_tasks(kind, t, s):
            rows.append([])
            for task in part:
                rows[-1].append((task, job))
                job += task[0] in BANK
        out.append((t, s, *rows))
    return out, job


FIRST, J0 = body("first")
LOOP, J = body("loop")
TAIL, _ = body("tail")
BODIES = {"first": FIRST, "loop": LOOP, "tail": TAIL}
JB, JB_TAIL = 2, 4
assert J % JB == 0 and (J0 + (NB - 1) * J) % JB == 0


def job_of(kind, b, pos):
    return pos if kind == "first" else b * J + (J0 - J + pos)


def bank_of(kind, pos):
    return pos % JB_TAIL if kind == "tail" else (pos if kind == "first" else J0 + pos) % JB


def bank_turn(kind, b, pos):
    if kind == "tail":
        return pos // JB_TAIL + ((J0 + (NB - 1) * J) // JB if pos % JB_TAIL < JB else 0)
    return pos // JB if kind == "first" else b * (J // JB) + ((J0 + pos) // JB - J // JB)


def at(kind, t, task):
    return next(pos for tt, _, early, late in BODIES[kind] for k, pos in early + late if tt == t and k == task)


def build(nc, x, tok_e, tok_t, fc1_w, fc2_w, exp_w, exp_b, W1, biases, out):
    f32, f32r, i32 = mybir.dt.float32, mybir.dt.float32r, mybir.dt.int32
    ALU, ACT, AX = mybir.AluOpType, mybir.ActivationFunctionType, mybir.AxisListType

    ctx = ExitStack()
    with ctx:
        def sb(name, shape, dt=f32):
            return ctx.enter_context(nc.sbuf_tensor(name, shape, dt))

        def pb(name):
            return ctx.enter_context(nc.psum_tensor(name, [P, 512], f32))

        def sem(name):
            return ctx.enter_context(nc.semaphore(name))

        w1T = sb("w1T", [P, HC, D])
        w2T = sb("w2T", [P, HC, D])
        w1h, w1l = sb("w1h", [P, 2, D], f32r), sb("w1l", [P, 2, D], f32r)
        w2h, w2l = sb("w2h", [P, 2, D], f32r), sb("w2l", [P, 2, D], f32r)
        xh = [sb(f"xh{i}", [P, DC, TT], f32r) for i in range(2)]
        xl = [sb(f"xl{i}", [P, DC, TT], f32r) for i in range(2)]
        x1T = sb("x1T", [P, OC, TT])
        raw = sb("raw", [P, DC, TT])
        g = sb("g", [P, 2, TT])
        hh, hl = sb("hh", [P, 2, TT], f32r), sb("hl", [P, 2, TT], f32r)
        xnh, xnl = sb("xnh", [P, CH, D], f32r), sb("xnl", [P, CH, D], f32r)
        W1h, W1l = sb("W1h", [P, DC, A], f32r), sb("W1l", [P, DC, A], f32r)
        Ph, Pl = sb("Ph", [P, CH, P], f32r), sb("Pl", [P, CH, P], f32r)
        Ws = sb("Ws", [P, CH, P], f32r)
        E4 = sb("E4", [P, CH, P], f32r)
        Bs = sb("Bs", [P, D], f32r)
        B1s = sb("B1s", [P, 2], f32r)
        th = sb("th", [P, TT])
        ident = sb("ident", [P, P])
        ones2 = sb("ones2", [P, 2], f32r)
        ones8 = sb("ones8", [CH, P])
        rep = sb("rep", [CH, GROUPS, 32])
        K0, KS, KP, KC = (sb(n, [P, MW]) for n in ("K0", "KS", "KP", "KC"))
        kt = sb("kt", [P, MW])
        TM = sb("TM", [P, MW])
        ty = sb("ty", [P, 1], i32)
        tyf = sb("tyf", [P, 4])
        cnti = sb("cnti", [P, 2 * CH], i32)
        bcol = sb("bcol", [P, NBR])
        vz = sb("vz", [P, CH, CH])
        s8a, s8 = sb("s8a", [CH, P]), sb("s8", [CH, P])
        F8, G8 = sb("F8", [CH, P + 1]), sb("G8", [CH, P + 1])
        DG = sb("DG", [CH, CH])
        st = sb("st", [P, 2 * CH + 1])
        t88, m0 = sb("t88", [CH, CH]), sb("m0", [CH, P])
        mc = sb("mc", [CH, 1])
        m8 = sb("m8", [CH, P])
        Ef = sb("Ef", [P, CH])
        E1 = sb("E1", [P, GROUPS, 32], f32r)
        rd = sb("rd", [P, CH])

        Pf = x1T[:, 0:2, :].rearrange("p a n -> p (a n)")
        oo = x1T
        xfull, last_rows = w1T[:, 0:CH, :], w1T[:, CH:2 * CH, :]
        Wf = x1T[:, 2:4, :].rearrange("p a n -> p (a n)")

        yb = [pb(f"y{i}") for i in range(OC)]
        hb = [pb(f"h{i}") for i in range(2)]
        jb = [pb(f"j{i}") for i in range(JB)] + hb

        raw_in = [sem(f"raw_in{i}") for i in range(DC)]
        w1_in = [sem(f"w1_in{i}") for i in range(len(W1_LOADS))]
        w2_in, exp_in = [sem(f"w2_in{q}") for q in range(4)], [sem(f"exp_in{q}") for q in range(4)]
        bias_in, W1_in, type_in = sem("bias_in"), sem("W1_in"), sem("type_in")
        out_put = [sem(f"out_put{i}") for i in range(OUTS)]
        const_done, mask_done = sem("const_done"), sem("mask_done")
        gstep = sem("gstep")
        vz_done = sem("vz_done")
        job_done = sem("job_done")
        bank_read = [sem(f"bank_read{i}") for i in range(JB_TAIL)]
        fc1_done, fc2_done = sem("fc1_done"), sem("fc2_done")
        w1hi, w1lo, w2hi, w2lo = sem("w1hi"), sem("w1lo"), sem("w2hi"), sem("w2lo")
        W1hi, W1lo = sem("W1hi"), sem("W1lo")
        gelu_done, hhi, hlo = sem("gelu_done"), sem("hhi"), sem("hlo")
        xhi, xlo, xnhi = sem("xhi"), sem("xlo"), sem("xnhi")
        ysum, x1_done, x1hi, x1lo = sem("ysum"), sem("x1_done"), sem("x1hi"), sem("x1lo")
        chain = sem("chain")
        exp_done = sem("exp_done")
        passed = sem("passed")
        Ehi, Elo = sem("Ehi"), sem("Elo")
        PWhi, Plo, Wlo = sem("PWhi"), sem("Plo"), sem("Wlo")
        sumhi = sem("sumhi")
        rd_done, row_sum, xfull_done = sem("rd_done"), sem("row_sum"), sem("xfull_done")

        NCHAIN, DIAG = 10, 3

        def wait(eng, s, value):
            if not (isinstance(value, int) and value <= 0):
                eng.wait_ge(s, value)

        def wait_used(eng, kind, b, pos):
            eng.wait_ge(bank_read[bank_of(kind, pos)], bank_turn(kind, b, pos) + 1)

        def gate(eng, s, value):
            wait(eng, s, value)
            eng.sem_inc(passed, 1)

        def run(eng, part):
            part("first", 0)
            with eng.Fori(1, NB) as b:
                part("loop", b)
            part("tail", NB)

        def slot_no(b, t, s):
            return b * 2 * HC + (t * HC + s)

        def tile_before(b, t):
            return b * 2 + (t - 1)

        def batch_of(ap, b):
            return ap[bass.ds(b, 1)]

        block = ctx.enter_context(nc.Block())

        @block.sync
        def _(sp):
            def load_x(kind, b, t, dc):
                rows = batch_of(x, (b + t) % NB)
                gate(sp, xlo, (b * 2 + t) * DC + (dc + 1))
                sp.dma_start(raw[:, dc, :], rows[:, dc * P:(dc + 1) * P, (1 - t) * TT:(2 - t) * TT].rearrange("o p n -> (o p) n")
                             ).then_inc(raw_in[dc], 16)

            def load_expert(e, q):
                sp.dma_start(w2T[:, 4 * q:4 * q + 4, SHARED:OC * P],
                             batch_of(exp_w, e)[:, :, 4 * q:4 * q + 4, :].rearrange("o p c n -> (o p) c n")
                             ).then_inc(exp_in[q], 16)

            def expert_of(b):
                return sp.value_load(batch_of(tok_e, b).rearrange("(o n) -> o n", o=1), min_val=0, max_val=exp_w.shape[0] - 1)

            def part(kind, b):
                if kind != "first":
                    sp.dma_start(ty[:, :], batch_of(tok_t, b - 1).rearrange("(o n) -> o n", o=1).to_broadcast([P, 1])
                                 ).then_inc(type_in, 16)
                for t, s, early, late in BODIES[kind]:
                    if s == 0 and kind != "tail":
                        for dc in range(DC):
                            load_x(kind, b, t, dc)
                    for task, pos in early + late:
                        if task[0] == "pool":
                            c = task[1]
                            rows = last_rows[:, c, :] if kind == "tail" else oo[:, c % OUTS, :]
                            if kind == "tail":
                                sp.wait_ge(bank_read[bank_of(kind, pos)], bank_turn(kind, b, pos) + 1)
                            else:
                                gate(sp, row_sum, b * CH + (c + 1 - CH))
                            sp.dma_start(batch_of(out, b - 1)[:, c * P:(c + 1) * P, :].rearrange("o p n -> (o p) n"), rows
                                         ).then_inc(out_put[c % OUTS], 16)
                    if t == 1 and s == 0:
                        e = expert_of((b + 1) % NB)
                    if t == 1 and s % 4 == 3:
                        gate(sp, w2lo, slot_no(b, t, s) + 1)
                        load_expert(e, s // 4)

            def load_w1(n):
                lo_, hi_ = W1_LOADS[n]
                sp.dma_start(w1T[:, lo_:hi_, :], fc1_w[:, lo_:hi_, :]).then_inc(w1_in[n], 16)

            def load_w2(q):
                sp.dma_start(w2T[:, 4 * q:4 * q + 4, 0:SHARED], fc2_w[:, 4 * q:4 * q + 4, :]).then_inc(w2_in[q], 16)

            for dc in range(DC):
                sp.dma_start(raw[:, dc, :], x[0:1, dc * P:(dc + 1) * P, 0:TT].rearrange("o p n -> (o p) n")
                             ).then_inc(raw_in[dc], 16)
                if dc == 0:
                    load_w1(0)
            load_w1(1)
            e = expert_of(0)
            load_w2(0)
            load_expert(e, 0)
            load_w1(2)
            load_w1(3)
            for q in range(1, 4):
                load_w2(q)
                load_expert(e, q)
                if q < 3:
                    load_w1(3 + q)
            sp.dma_start(x1T[:, 0, :], W1).then_inc(W1_in, 16)
            run(sp, part)
            for i in range(OUTS):
                sp.wait_ge(out_put[i], 16 * NB * CH // OUTS)
            for i in range(DC):
                sp.wait_ge(raw_in[i], 16 * (2 * NB + 1))
            for q in range(4):
                sp.wait_ge(exp_in[q], 16 * (NB + 1))

        @block.gpsimd
        def _(pool):
            steps = [0]

            def link(ins):
                steps[0] += 1
                ins.then_inc(gstep, 1)
                pool.wait_ge(gstep, steps[0])

            def mark(ap, coef, count, cm, base=0, equal=False, fill=NEG):
                k = 1 if equal else -1
                return nc.gpsimd.affine_select(
                    out=ap, in_=ap, compare_op=ALU.not_equal if equal else ALU.is_ge, fill=fill,
                    base=k * base, pattern=[[k * coef, count]], channel_multiplier=k * cm)

            link(nc.gpsimd.memset(ident[:, :], 0.0))
            mark(ident[:, :], -1, P, 1, equal=True, fill=1.0).then_inc(const_done, 1)
            pool.wait_ge(const_done, 1)
            pool.dma_start(bcol[:, 0:NFIX], biases).then_inc(bias_in, 16)
            for b in range(NB):
                e = pool.value_load(tok_e[b:b + 1].rearrange("(o n) -> o n", o=1), min_val=0, max_val=exp_b.shape[0] - 1)
                pool.dma_start(bcol[:, R_EXP + b:R_EXP + b + 1], batch_of(exp_b, e).rearrange("o p -> p o")).then_inc(bias_in, 16)
            link(nc.gpsimd.memset(ones8[:, :], 1.0))
            link(nc.gpsimd.memset(ones2[:, :].bitcast(f32), 1.0))
            link(nc.gpsimd.memset(vz[:, :, :], 0.0))
            link(nc.gpsimd.memset(E4[:, :, :].bitcast(f32), 0.0))
            link(nc.gpsimd.memset(E1[:, :, :].bitcast(f32), 0.0))
            link(nc.gpsimd.memset(F8[:, :], NEG))
            link(nc.gpsimd.memset(G8[:, :], NEG))
            for tile in (K0, KS, KP):
                link(nc.gpsimd.memset(tile[:, :], 0.0))
            link(nc.gpsimd.memset(KC[:, :], 0.0))
            for gr in range(GROUPS):
                link(nc.gpsimd.tensor_copy(rep[:, gr, :], ident[0:CH, 0:32]))
            link(mark(KS[:, TRI], 1, P, -1))
            link(mark(KP[:, TRI], -1, P, 1))
            link(mark(KC[:, TRI], -1, P, 1, equal=True))
            for gr in range(GROUPS):
                rows = slice(32 * gr, 32 * gr + 32)
                link(mark(KS[rows, CROSS], 1, CH, -1))
                link(mark(KP[rows, CROSS], -1, CH, 1))
                link(mark(K0[rows, CROSS], -1, CH, 1, equal=True))
                link(mark(K0[rows, CROSS], 0, CH, 1, base=1 - CH))
            link(mark(KS[:, SEEN], -1, CH, 1))
            link(mark(KP[:, SEEN], 1, CH, -1))
            link(mark(K0[:, SEEN], -1, CH, 1, equal=True))
            link(nc.gpsimd.memset(KS[:, NS:NS + 1], NEG))
            link(nc.gpsimd.memset(KP[:, NP_:NP_ + 1], NEG))
            link(nc.gpsimd.memset(KC[:, NC:NC + 1], NEG))
            link(nc.gpsimd.memset(KC[:, CNT], float(SEQ - 1)))
            link(nc.gpsimd.iota(cnti[:, 0:CH], pattern=[[-P, CH]], base=SEQ, channel_multiplier=-1))
            link(nc.gpsimd.iota(cnti[:, CH:2 * CH], pattern=[[P, CH]], base=1, channel_multiplier=1))
            link(nc.gpsimd.tensor_copy(KS[:, CNT], cnti[:, 0:CH]))
            link(nc.gpsimd.tensor_copy(KP[:, CNT], cnti[:, CH:2 * CH]))
            nc.gpsimd.memset(kt[:, 0:1], 0.0).then_inc(const_done, 1)
            before_masks, per_mask = steps[0], 10

            def part(kind, b):
                if kind == "first":
                    return
                made = [0]

                def then(ins):
                    made[0] += 1
                    ins.then_inc(gstep, 1)
                    gate(pool, gstep, b * per_mask + (before_masks - per_mask + made[0]))

                gate(pool, type_in, b * 16)
                then(nc.gpsimd.tensor_copy(tyf[:, 0:1], ty[:, :]))
                then(nc.gpsimd.tensor_scalar(tyf[:, 1:2], tyf[:, 0:1], 0.0, None, ALU.is_equal))
                then(nc.gpsimd.tensor_scalar(tyf[:, 2:3], tyf[:, 0:1], 1.0, None, ALU.is_equal))
                then(nc.gpsimd.tensor_tensor(tyf[:, 3:4], tyf[:, 1:2], tyf[:, 2:3], ALU.add))
                then(nc.gpsimd.tensor_scalar(tyf[:, 3:4], tyf[:, 3:4], -1.0, 1.0, ALU.mult, ALU.add))
                then(nc.gpsimd.tensor_scalar(kt[:, :], KS[:, :], tyf[:, 2:3], None, ALU.mult))
                then(nc.gpsimd.tensor_scalar(TM[:, :], KP[:, :], tyf[:, 1:2], None, ALU.mult))
                then(nc.gpsimd.tensor_tensor(TM[:, :], TM[:, :], kt[:, :], ALU.add))
                then(nc.gpsimd.tensor_scalar(kt[:, :], KC[:, :], tyf[:, 3:4], None, ALU.mult))
                then(nc.gpsimd.tensor_tensor(TM[:, :], TM[:, :], kt[:, :], ALU.add))
                nc.gpsimd.tensor_tensor(TM[:, :], TM[:, :], K0[:, :], ALU.add).then_inc(mask_done, 1)
                if kind == "tail":
                    for c in range(CH):
                        wait_used(pool, kind, b, at(kind, 0, ("xn", c % CT)) if c >= CT else at(kind, 0, ("xn", 0)))
                        nc.gpsimd.tensor_tensor(xfull[:, c, :], xnh[:, c, :].bitcast(f32), xnl[:, c, :].bitcast(f32),
                                                ALU.add).then_inc(xfull_done, 1)
                    return
                for t, s, early, late in BODIES[kind]:
                    for task, pos in early + late:
                        if task[0] == "pool":
                            c = task[1]
                            wait_used(pool, kind, b, pos)
                            nc.gpsimd.tensor_tensor(oo[:, c % OUTS, :], oo[:, c % OUTS, :], xnl[:, c, :].bitcast(f32),
                                                    ALU.add).then_inc(row_sum, 1)

            run(pool, part)

        @block.tensor
        def _(pe):
            def three(ps, ah, al, bh, bl, first, last):
                nc.tensor.matmul(ps, ah, bh, start=first, stop=False)
                nc.tensor.matmul(ps, ah, bl, start=False, stop=False)
                return nc.tensor.matmul(ps, al, bh, start=False, stop=last)

            def fc1(kind, b, t, s):
                ring, S = s % 2, slot_no(b, t, s)
                pe.wait_ge(w1lo, S + 1)
                wait(pe, gelu_done, S - 1)
                for dc in range(DC):
                    if s == 0:
                        pe.wait_ge(xlo, (b * 2 + t) * DC + (dc + 1))
                    w = slice(dc * P, (dc + 1) * P)
                    last = three(hb[ring][:, :], w1h[:, ring, w], w1l[:, ring, w], xh[t][:, dc, :], xl[t][:, dc, :],
                                 dc == 0, dc == DC - 1)
                last.then_inc(fc1_done, 1)

            def fc2(b, t, s):
                ring, S = s % 2, slot_no(b, t, s)
                pe.wait_ge(w2lo, S + 1)
                pe.wait_ge(hlo, S + 1)
                for oc in range(OC):
                    if s == 0:
                        wait(pe, ysum, tile_before(b, t) * OC + (oc + 1))
                    w = slice(oc * P, (oc + 1) * P)
                    three(yb[oc][:, :], w2h[:, ring, w], w2l[:, ring, w], hh[:, ring, :], hl[:, ring, :],
                          s == 0, s == HC - 1).then_inc(fc2_done, 1)

            def job(kind, b, t, task, pos):
                if task[0] not in BANK:
                    return
                bank = jb[bank_of(kind, pos)]
                T1 = tile_before(b, t)
                wait(pe, bank_read[bank_of(kind, pos)], bank_turn(kind, b, pos))
                if task[0] == "xn":
                    c = task[1]
                    pe.wait_ge(x1_done, T1 * OC + OC)
                    for i in range(OC):
                        last = nc.tensor.transpose(bank[:, i * P:(i + 1) * P], x1T[:, i, c * P:(c + 1) * P], ident[:, :])
                elif task[0] == "attn":
                    if kind == "first":
                        pe.wait_ge(W1lo, 1)
                    for dc in range(DC):
                        pe.wait_ge(x1lo, T1 * OC + (dc + 1))
                        last = three(bank[:, :], W1h[:, dc, :], W1l[:, dc, :], xh[1 - t][:, dc, :], xl[1 - t][:, dc, :],
                                     dc == 0, dc == DC - 1)
                elif task[0] == "score":
                    wait_used(pe, kind, b, at(kind, t, ("attn",)))
                    if kind == "first":
                        pe.wait_ge(vz_done, 1)
                    for i in range(CT):
                        last = nc.tensor.matmul(bank[0:CH, 0:P], vz[:, (1 - t) * CT + i, :], th[:, i * P:(i + 1) * P],
                                                start=(i == 0), stop=(i == CT - 1))
                elif task[0] == "stats":
                    pe.wait_ge(chain, b * NCHAIN + (DIAG - NCHAIN))
                    nc.tensor.matmul(bank[:, CH:2 * CH], ones8[:, :], DG[:, :], start=True, stop=True)
                    nc.tensor.transpose(bank[:, 0:CH], s8[:, :], ident[0:CH, 0:CH])
                    last = nc.tensor.matmul(bank[:, 2 * CH:2 * CH + 1], rep[:, :, :].rearrange("c g k -> c (g k)"),
                                            F8[:, P:P + 1], start=True, stop=True)
                elif task[0] == "bc":
                    pe.wait_ge(chain, b * NCHAIN)
                    for i in range(CT):
                        c = task[1] * CT + i
                        last = nc.tensor.matmul(bank[:, i * P:(i + 1) * P], ident[0:CH, c:c + 1].to_broadcast([CH, P]),
                                                m8[:, :], start=True, stop=True)
                elif task[0] == "sums":
                    pe.wait_ge(Elo, b)
                    wait_used(pe, kind, b, at(kind, t, ("xn", CT - 1)))
                    for c in range(CH):
                        nc.tensor.matmul(bank[:, :], E4[:, c, :], xnh[:, c, :], start=(c == 0), stop=False)
                        last = nc.tensor.matmul(bank[:, :], E4[:, c, :], xnl[:, c, :], start=False, stop=(c == CH - 1))
                elif task[0] == "sums1":
                    last = nc.tensor.matmul(bank[:, 0:2], E1[:, :, :].rearrange("p g c -> p (g c)"), ones2[:, :],
                                            start=True, stop=True)
                elif task[0] == "den":
                    _, c0, c1 = task
                    pe.wait_ge(Plo, b * 2 + (c1 // BC - 2))
                    pe.wait_ge(Wlo, b * 2 + (c1 // BC - 2))
                    wait_used(pe, kind, b, at(kind, t, ("sums1",)))
                    for c in range(c0, c1):
                        two = bank[:, 2 * c:2 * c + 2]
                        nc.tensor.matmul(two, Ph[:, c, :], ones2[:, :], start=True, stop=False)
                        nc.tensor.matmul(two, Pl[:, c, :], ones2[:, :], start=False, stop=False)
                        last = nc.tensor.matmul(two, Ws[:, c, :], B1s[:, :], start=False, stop=True)
                elif task[0] == "pool":
                    c = task[1]
                    three(bank[:, :], Ph[:, c, :], Pl[:, c, :], xnh[:, c, :], xnl[:, c, :], True, False)
                    last = nc.tensor.matmul(bank[:, :], Ws[:, c, :], Bs[:, :], start=False, stop=True)
                last.then_inc(job_done, 1)

            def part(kind, b):
                for t, s, early, late in BODIES[kind]:
                    if kind != "tail":
                        fc1(kind, b, t, s)
                    for task, pos in early:
                        job(kind, b, t, task, pos)
                    if s > 0:
                        fc2(b, t, s - 1)
                    elif t == 1:
                        fc2(b, 0, HC - 1)
                    elif kind != "first":
                        fc2(b - 1, 1, HC - 1)
                    for task, pos in late:
                        job(kind, b, t, task, pos)

            pe.wait_ge(const_done, 1)
            run(pe, part)

        @block.scalar
        def _(act):
            def hi(out_, in_):
                return nc.scalar.activation(out_, in_, ACT.Copy)

            def split_w1(kind, b, t, s):
                nxt, S1 = (s + 1) % HC, slot_no(b, t, s + 1)
                first_use = [lo_ for lo_, _ in W1_LOADS]
                if kind == "first" and t == 0 and nxt in first_use:
                    act.wait_ge(w1_in[first_use.index(nxt)], 16)
                wait(act, fc1_done, S1 - 1)
                hi(w1h[:, nxt % 2, :], w1T[:, nxt, :]).then_inc(w1hi, 1)

            def split_w2(kind, b, t, s):
                if t == 0 and s % 4 == 0:
                    if kind == "first":
                        act.wait_ge(w2_in[s // 4], 16)
                    act.wait_ge(exp_in[s // 4], b * 16 + 16)
                wait(act, fc2_done, (slot_no(b, t, s) - 2) * OC + OC)
                hi(w2h[:, s % 2, :], w2T[:, s, :]).then_inc(w2hi, 1)

            def task_part(kind, b, t, task, pos):
                T1 = tile_before(b, t)
                bank = jb[bank_of(kind, pos)]
                if task[0] in ("xn", "attn", "sums", "sums1"):
                    act.wait_ge(job_done, job_of(kind, b, pos) + 1)
                if task[0] == "x":
                    dc = task[1]
                    act.wait_ge(raw_in[dc], (b * 2 + t) * 16 + 32)
                    hi(xh[1 - t][:, dc, :], raw[:, dc, :]).then_inc(xhi, 1)
                elif task[0] == "x1":
                    oc = task[1]
                    act.wait_ge(x1_done, T1 * OC + (oc + 1))
                    hi(xh[1 - t][:, oc, :], x1T[:, oc, :]).then_inc(x1hi, 1)
                elif task[0] == "xn":
                    if task[1] == 0 and t == 1 and kind == "loop":
                        wait_used(act, kind, b, at(kind, 0, ("pool", CH - 1)))
                    hi(xnh[:, (1 - t) * CT + task[1], :], bank[:, :]).then_inc(xnhi, 1)
                elif task[0] == "attn":
                    nc.scalar.activation(th[:, :], bank[:, :], ACT.Tanh, bias=bcol[:, R_B1:R_B1 + 1]
                                         ).then_inc(bank_read[bank_of(kind, pos)], 1)
                elif task[0] == "expE":
                    act.wait_ge(chain, b * NCHAIN + (DIAG + 1 - NCHAIN))
                    nc.scalar.activation(Ef[:, :], Ef[:, :], ACT.Exp).then_inc(exp_done, 1)
                elif task[0] == "expPW":
                    h = task[1]
                    wait_used(act, kind, b, at(kind, t, ("bc", h)))
                    half, cs = slice(h * TT, (h + 1) * TT), slice(h * BC, (h + 1) * BC)
                    for tile in (Pf, Wf):
                        nc.scalar.activation(tile[:, half], tile[:, half], ACT.Exp).then_inc(exp_done, 1)
                    for i, (part_, full) in enumerate(((Ph, Pf), (Ws, Wf))):
                        act.wait_ge(exp_done, b * 5 + (2 * h + i - 3))
                        hi(part_[:, cs, :].rearrange("p c n -> p (c n)"), full[:, half]).then_inc(PWhi, 1)
                elif task[0] == "sums":
                    hi(Bs[:, :], bank[:, :]).then_inc(sumhi, 1)
                elif task[0] == "sums1":
                    hi(B1s[:, :], bank[:, 0:2]).then_inc(sumhi, 1)

            def part(kind, b):
                for t, s, early, late in BODIES[kind]:
                    if kind != "tail":
                        S, ring = slot_no(b, t, s), s % 2
                        split_w1(kind, b, t, s)
                        act.wait_ge(fc1_done, S + 1)
                        wait(act, hlo, S - 1)
                        if kind == "first" and t == 0 and s == 0:
                            act.wait_ge(bias_in, 16 * (1 + NB))
                        nc.scalar.activation(g[:, ring, :], hb[ring][:, :], ACT.Gelu,
                                             bias=bcol[:, R_FC1 + s:R_FC1 + s + 1]).then_inc(gelu_done, 1)
                        wait(act, fc2_done, (S - 2) * OC + OC)
                        act.wait_ge(gelu_done, S + 1)
                        hi(hh[:, ring, :], g[:, ring, :]).then_inc(hhi, 1)
                        split_w2(kind, b, t, s)
                    if kind == "first" and t == 0 and s == HC // 2:
                        act.wait_ge(W1_in, 16)
                        hi(W1h[:, :, :].rearrange("p c a -> p (c a)"), x1T[:, 0, :]).then_inc(W1hi, 1)
                    for task, pos in early + late:
                        task_part(kind, b, t, task, pos)

            for dc in range(DC):
                act.wait_ge(raw_in[dc], 16)
                hi(xh[0][:, dc, :], raw[:, dc, :]).then_inc(xhi, 1)
                if dc == 0:
                    act.wait_ge(w1_in[0], 16)
                    hi(w1h[:, 0, :], w1T[:, 0, :]).then_inc(w1hi, 1)
            run(act, part)

        @block.vector
        def _(dve):
            def lo(out_, in_, hi_):
                return nc.vector.tensor_tensor(out_, in_, hi_.bitcast(f32), ALU.subtract)

            def task_part(kind, b, t, task, pos):
                T1 = tile_before(b, t)
                bk = bank_of(kind, pos)
                bank, used = jb[bk], bank_read[bk]
                if task[0] in ("score", "stats", "bc", "den", "pool"):
                    dve.wait_ge(job_done, job_of(kind, b, pos) + 1)
                if task[0] == "x":
                    dc = task[1]
                    dve.wait_ge(xhi, (b * 2 + t) * DC + (DC + dc + 1))
                    lo(xl[1 - t][:, dc, :], raw[:, dc, :], xh[1 - t][:, dc, :]).then_inc(xlo, 1)
                elif task[0] == "ysum":
                    oc = task[1]
                    bias = (bcol[:, R_FC2 + oc:R_FC2 + oc + 1] if oc < OC - 1 else
                            bcol[:, bass.ds(b + (R_EXP + t - 1), 1)])
                    if t == 1 and kind == "loop":
                        dve.wait_ge(out_put[oc], b * (16 * CH // OUTS))
                    if kind == "first":
                        dve.wait_ge(W1lo, 1)
                    dve.wait_ge(fc2_done, T1 * HC * OC + ((HC - 1) * OC + oc + 1))
                    nc.vector.scalar_tensor_tensor(x1T[:, oc, :], yb[oc][:, :], bias, xh[1 - t][:, oc, :].bitcast(f32),
                                                   ALU.add, ALU.add).then_inc(ysum, 1)
                elif task[0] == "x1":
                    oc = task[1]
                    dve.wait_ge(ysum, T1 * OC + (oc + 1))
                    nc.vector.tensor_tensor(x1T[:, oc, :], x1T[:, oc, :], xl[1 - t][:, oc, :].bitcast(f32),
                                            ALU.add).then_inc(x1_done, 1)
                elif task[0] == "x1lo":
                    oc = task[1]
                    dve.wait_ge(x1hi, T1 * OC + (oc + 1))
                    lo(xl[1 - t][:, oc, :], x1T[:, oc, :], xh[1 - t][:, oc, :]).then_inc(x1lo, 1)
                elif task[0] == "xn":
                    c = (1 - t) * CT + task[1]
                    dve.wait_ge(xnhi, T1 * CT + (task[1] + 1))
                    if task[1] == 0 and t == 1 and kind == "loop":
                        dve.wait_ge(row_sum, b * CH)
                    lo(xnl[:, c, :], bank[:, :], xnh[:, c, :]).then_inc(used, 1)
                elif task[0] == "score":
                    if t == 1:
                        nc.vector.tensor_copy(s8a[:, :], bank[0:CH, 0:P]).then_inc(used, 1)
                    else:
                        nc.vector.tensor_tensor(s8[:, :], bank[0:CH, 0:P], s8a[:, :], ALU.add).then_inc(used, 1)
                        wait_used(dve, kind, b, pos)
                        maxima(b)
                elif task[0] == "stats":
                    nc.vector.tensor_copy(st[:, :], bank[:, 0:2 * CH + 1]).then_inc(used, 1)
                    dve.wait_ge(mask_done, b)
                    wait_used(dve, kind, b, pos)
                    row_maxima(b)
                elif task[0] == "bc":
                    for i in range(CT):
                        c = task[1] * CT + i
                        nc.vector.scalar_tensor_tensor(Pf[:, c * P:(c + 1) * P], bank[:, i * P:(i + 1) * P], st[:, c:c + 1],
                                                       TM[:, TRI], ALU.add, ALU.add)
                    half = slice(task[1] * TT, (task[1] + 1) * TT)
                    cross = TM[:, P + task[1] * CT:P + (task[1] + 1) * CT]
                    nc.vector.scalar_tensor_tensor(
                        Wf[:, half].rearrange("p (c n) -> p c n", c=CT), bank[:, :].rearrange("p (c n) -> p c n", c=CT),
                        st[:, 2 * CH:2 * CH + 1], cross.unsqueeze(2).to_broadcast([P, CT, P]), ALU.add, ALU.add
                    ).then_inc(used, 1)
                elif task[0] == "expE":
                    diagonal = E4[:, :, :].rearrange("p c n -> p (c n)")
                    dve.wait_ge(exp_done, b * 5 - 4)
                    nc.vector.tensor_copy(E1[:, 0:GROUPS - 1, 0:CH], Ef[:, :].unsqueeze(1).to_broadcast([P, GROUPS - 1, CH]))
                    for gr in range(GROUPS - 1):
                        last = nc.vector.tensor_copy(diagonal[:, 32 * gr:32 * gr + (CH - 1) * (P + 1) + 1:P + 1], Ef[:, :])
                    last.then_inc(Ehi, 1)
                    dve.wait_ge(Ehi, b)
                    gr = GROUPS - 1
                    lo(E1[:, gr, 0:CH], Ef[:, :], E1[:, 0, 0:CH])
                    lo(diagonal[:, 32 * gr:32 * gr + (CH - 1) * (P + 1) + 1:P + 1], Ef[:, :],
                       diagonal[:, 0:(CH - 1) * (P + 1) + 1:P + 1]).then_inc(Elo, 1)
                elif task[0] == "expPW":
                    h = task[1]
                    half, cs = slice(h * TT, (h + 1) * TT), slice(h * BC, (h + 1) * BC)
                    dve.wait_ge(PWhi, b * 4 + (2 * h - 3))
                    lo(Pl[:, cs, :].rearrange("p c n -> p (c n)"), Pf[:, half], Ph[:, cs, :].rearrange("p c n -> p (c n)")
                       ).then_inc(Plo, 1)
                    dve.wait_ge(PWhi, b * 4 + (2 * h - 2))
                    third = Ws[64:96, cs, :].rearrange("p c n -> p (c n)")
                    lo(third, Wf[64:96, half], third).then_inc(Wlo, 1)
                elif task[0] == "sums":
                    dve.wait_ge(sumhi, b * 2 - 1)
                    lo(Bs[32:64, :], bank[32:64, :], Bs[32:64, :]).then_inc(used, 1)
                elif task[0] == "sums1":
                    dve.wait_ge(sumhi, b * 2)
                    lo(B1s[32:64, :], bank[32:64, 0:2], B1s[32:64, :]).then_inc(used, 1)
                elif task[0] == "den":
                    cs = slice(task[1], task[2])
                    nc.vector.tensor_tensor(rd[:, cs], bank[:, 2 * task[1]:2 * task[2]].rearrange("p (c k) -> p c k", k=2)[:, :, 0],
                                            TM[:, CNT][:, cs], ALU.mult).then_inc(used, 1)
                    wait_used(dve, kind, b, pos)
                    nc.vector.reciprocal(rd[:, cs], rd[:, cs]).then_inc(rd_done, 1)
                elif task[0] == "pool":
                    c = task[1]
                    if c >= OUTS and kind != "tail":
                        dve.wait_ge(out_put[c % OUTS], b * (16 * CH // OUTS) + 16 * (c // OUTS - CH // OUTS))
                    if c == 0 or kind == "tail" and c == BC:
                        dve.wait_ge(rd_done, b + c // BC)
                    if kind == "tail":
                        dve.wait_ge(xfull_done, c + 1)
                        nc.vector.scalar_tensor_tensor(last_rows[:, c, :], bank[:, :], rd[:, c:c + 1], xfull[:, c, :],
                                                       ALU.mult, ALU.add).then_inc(used, 1)
                        return
                    nc.vector.scalar_tensor_tensor(oo[:, c % OUTS, :], bank[:, :], rd[:, c:c + 1], xnh[:, c, :].bitcast(f32),
                                                   ALU.mult, ALU.add).then_inc(used, 1)

            def link(ins, b, number):
                ins.then_inc(chain, 1)
                dve.wait_ge(chain, b * NCHAIN + (number - NCHAIN))

            def maxima(b):
                nc.vector.tensor_tensor_scan(G8[:, P - 1::-1], s8[:, P - 1::-1], s8[:, P - 1::-1], NEG, ALU.max, ALU.max
                                             ).then_inc(chain, 1)
                link(nc.vector.tensor_tensor_scan(F8[:, 1:P + 1], s8[:, :], s8[:, :], NEG, ALU.max, ALU.max), b, 2)
                nc.vector.tensor_scalar(DG[:, :], ident[0:CH, 0:CH], F8[:, P:P + 1], None, ALU.mult).then_inc(chain, 1)

            def row_maxima(b):
                nc.vector.tensor_tensor(Ef[:, :], st[:, 0:CH], st[:, CH:2 * CH], ALU.subtract).then_inc(chain, 1)
                link(nc.vector.tensor_tensor(t88[:, :], st[0:CH, CH:2 * CH], TM[0:CH, SEEN], ALU.add), b, 5)
                nc.vector.reduce_max(mc[:, :], t88[:, :], AX.X).then_inc(chain, 1)
                link(nc.vector.tensor_scalar(m0[:, :], s8[:, :], TM[0:CH, NC:NC + 1], None, ALU.add), b, 7)
                link(nc.vector.scalar_tensor_tensor(m0[:, :], G8[:, 1:P + 1], TM[0:CH, NP_:NP_ + 1], m0[:, :],
                                                    ALU.add, ALU.max), b, 8)
                link(nc.vector.scalar_tensor_tensor(m0[:, :], F8[:, 0:P], TM[0:CH, NS:NS + 1], m0[:, :],
                                                    ALU.add, ALU.max), b, 9)
                nc.vector.tensor_scalar(m8[:, :], m0[:, :], mc[:, :], -1.0, ALU.max, ALU.mult).then_inc(chain, 1)

            def part(kind, b):
                for t, s, early, late in BODIES[kind]:
                    if kind == "first" and t == 1 and s == 0:
                        dve.wait_ge(const_done, 2)
                        diagonal = vz[:, :, :].rearrange("p c n -> p (c n)")
                        nc.vector.tensor_copy(diagonal[:, ::CH + 1], bcol[:, R_V:R_V + 1].to_broadcast([P, CH])
                                              ).then_inc(vz_done, 1)
                    if kind != "tail":
                        S, ring = slot_no(b, t, s), s % 2
                        nxt = (s + 1) % HC
                        dve.wait_ge(w1hi, S + 2)
                        lo(w1l[:, nxt % 2, :], w1T[:, nxt, :], w1h[:, nxt % 2, :]).then_inc(w1lo, 1)
                        dve.wait_ge(hhi, S + 1)
                        lo(hl[:, ring, :], g[:, ring, :], hh[:, ring, :]).then_inc(hlo, 1)
                        split_w2(S, s)
                    if kind == "first" and t == 0 and s == HC // 2:
                        dve.wait_ge(W1hi, 1)
                        lo(W1l[:, :, :].rearrange("p c a -> p (c a)"), x1T[:, 0, :], W1h[:, :, :].rearrange("p c a -> p (c a)")
                           ).then_inc(W1lo, 1)
                    for task, pos in early + late:
                        task_part(kind, b, t, task, pos)

            def split_w2(S, s):
                dve.wait_ge(w2hi, S + 1)
                lo(w2l[:, s % 2, :], w2T[:, s, :], w2h[:, s % 2, :]).then_inc(w2lo, 1)

            for dc in range(DC):
                dve.wait_ge(xhi, dc + 1)
                lo(xl[0][:, dc, :], raw[:, dc, :], xh[0][:, dc, :]).then_inc(xlo, 1)
                if dc == 0:
                    dve.wait_ge(w1hi, 1)
                    lo(w1l[:, 0, :], w1T[:, 0, :], w1h[:, 0, :]).then_inc(w1lo, 1)
            run(dve, part)


def kernel(**inputs):
    import numpy as np
    import concourse.bacc as bacc
    from concourse.bass_utils import run_bass_kernel_spmd

    by = {name: np.asarray(a) for name, a in inputs.items()}
    columns = lambda a: a.reshape(-1, P).T
    fc1_w = by["L0_cond_fc1_w"].reshape(HC, P, DC, P).transpose(3, 0, 2, 1).reshape(P, HC, D)
    fc2_w = by["L0_cond_fc2_w"].reshape(SHARED, HC, P).transpose(2, 1, 0)
    exp_w = by["L0_cond_experts_w"].reshape(-1, PART, HC, P).transpose(0, 3, 2, 1)
    laid_out = {
        "x": by["x"].transpose(0, 2, 1), "itok_B_0_15": by["itok_B_0_15"], "itok_B_0_2": by["itok_B_0_2"],
        "fc1_w": fc1_w, "fc2_w": fc2_w, "experts_w": exp_w, "experts_b": by["L0_cond_experts_b"],
        "W1": by["L1_cond_W1"].reshape(DC, P, A).transpose(1, 0, 2).reshape(P, DC * A),
        "biases": np.concatenate([columns(by[n]) for n in ("L0_cond_fc1_b", "L0_cond_fc2_b", "L1_cond_b1", "L1_cond_v")], 1),
    }
    nc = bacc.Bacc("TRN2", target_bir_lowering=False, num_devices=1)
    arrays, args = {}, []
    for name, a in laid_out.items():
        a = np.ascontiguousarray(a)
        arrays[f"in_{name}"] = a
        args.append(nc.dram_tensor(f"in_{name}", a.shape, mybir.dt.from_np(a.dtype), kind="ExternalInput").ap())
    args.append(nc.dram_tensor("out_x", (NB, SEQ, D), mybir.dt.float32, kind="ExternalOutput").ap())
    build(nc, *args)
    r = run_bass_kernel_spmd(nc, [arrays], core_ids=[0])
    return r.results[0]["out_x"]
```
